# Optimizing a Trainium2 kernel written in Bass

```python
import numpy as np
import jax
import jax.numpy as jnp

def _softmax(x, axis=-1):
    return jax.nn.softmax(x, axis=axis)

def _gelu(x):
    return jax.nn.gelu(x, approximate=True)

def _silu(x):
    return jax.nn.silu(x)

def _sigmoid(x):
    return jax.nn.sigmoid(x)

def _layernorm(x, axis=-1, eps=1e-05):
    m = jnp.mean(x, axis=axis, keepdims=True)
    v = jnp.var(x, axis=axis, keepdims=True)
    return (x - m) / jnp.sqrt(v + eps)

def _scatter_add(tgt, idx, src, axis=0):
    return tgt.at[idx].add(src)

def _segment_sum(src, seg, n):
    return jax.ops.segment_sum(src, seg, n)
kernel_name = 'mk_decoder_preln_d2_seqx_r8_31abae'

def setup_inputs(seed: int=0):
    np.random.seed(seed)
    _w = jnp.asarray

    def _rec_inputs():
        import jax
        import jax.numpy as jnp
        _rk = jax.random.key(seed)
        x = -0.0001661 + 0.9999 * jax.random.normal(jax.random.fold_in(_rk, 1), (4, 256, 128), jnp.float32)
        _lenS = 256 - jax.random.randint(jax.random.fold_in(_rk, 7), (4,), 0, max(1, 256 // 4) + 1, jnp.int32)
        _lenS2 = 1601 - jax.random.randint(jax.random.fold_in(_rk, 8), (4,), 0, max(1, 1601 // 4) + 1, jnp.int32)
        _ctx_1024P = jax.random.normal(jax.random.fold_in(_rk, 11), (4, 16, 128), jnp.float32)
        _ctx_1024c = jax.random.dirichlet(jax.random.fold_in(_rk, 511), 0.3 * jnp.ones((16,), jnp.float32), (4, 1601))
        _ctx_1024t = jnp.einsum('bsk,bkd->bsd', _ctx_1024c, _ctx_1024P)
        _ctx_1024t = _ctx_1024t * jax.lax.rsqrt(jnp.mean(jnp.square(_ctx_1024t)) + 1e-12) * 0.953939
        ctx_1024 = -0.000119273 + 0.999915 * (_ctx_1024t + 0.3 * jax.random.normal(jax.random.fold_in(_rk, 611), (4, 1601, 128), jnp.float32))
        return (x, ctx_1024)
    x, ctx_1024 = _rec_inputs()

    def _L0_attn_setup():
        import jax, jax.numpy as jnp
        import numpy as np
        D_MODEL = 128
        NUM_HEADS = 16
        MAX_LEN = 256
        BATCH = 2
        SEQ_LEN = 256
        key = jax.random.key(seed)
        ks = jax.random.split(key, 6)
        s = 0.02
        return {'x': jax.random.normal(ks[0], (BATCH, SEQ_LEN, D_MODEL), dtype=jnp.float32), 'Wq': jax.random.normal(ks[1], (D_MODEL, D_MODEL), dtype=jnp.float32) * s, 'bq': jnp.zeros((D_MODEL,), dtype=jnp.float32), 'Wk': jax.random.normal(ks[2], (D_MODEL, D_MODEL), dtype=jnp.float32) * s, 'bk': jnp.zeros((D_MODEL,), dtype=jnp.float32), 'Wv': jax.random.normal(ks[3], (D_MODEL, D_MODEL), dtype=jnp.float32) * s, 'bv': jnp.zeros((D_MODEL,), dtype=jnp.float32), 'rel_emb': jax.random.normal(ks[4], (NUM_HEADS, 2 * MAX_LEN - 1), dtype=jnp.float32)}
    _L0_attn_all = _L0_attn_setup()
    _L0_attn_in = {k: v for k, v in _L0_attn_all.items() if k in ('Wq', 'bq', 'Wk', 'bk', 'Wv', 'bv', 'rel_emb')}
    del _L0_attn_all

    def _L0_xattn_setup():
        import jax, jax.numpy as jnp
        import numpy as np
        B, LQ, LK = (8, 256, 256)
        HIST_DIM, COMB_DIM, FUSION_DIM = (128, 128, 128)

        def _linear_params(key, in_dim, out_dim):
            k1, k2 = jax.random.split(key)
            bound = 1.0 / np.sqrt(in_dim)
            W = jax.random.uniform(k1, (out_dim, in_dim), jnp.float32, -bound, bound)
            b = jax.random.uniform(k2, (out_dim,), jnp.float32, -bound, bound)
            return (W, b)

        def _lin(x, W, b):
            return jnp.einsum('bld,fd->blf', x, W) + b
        key = jax.random.key(seed)
        ks = jax.random.split(key, 8)
        hW, hb = _linear_params(ks[0], HIST_DIM, FUSION_DIM)
        cW, cb = _linear_params(ks[1], COMB_DIM, FUSION_DIM)
        qW, qb = _linear_params(ks[2], FUSION_DIM, FUSION_DIM)
        kW, kb = _linear_params(ks[3], FUSION_DIM, FUSION_DIM)
        vW, vb = _linear_params(ks[4], FUSION_DIM, FUSION_DIM)
        oW, ob = _linear_params(ks[5], FUSION_DIM, FUSION_DIM)
        return {'history_features': jax.random.normal(ks[6], (B, LQ, HIST_DIM), jnp.float32), 'combined_features': jax.random.normal(ks[7], (B, LK, COMB_DIM), jnp.float32), 'hW': hW, 'hb': hb, 'cW': cW, 'cb': cb, 'qW': qW, 'qb': qb, 'kW': kW, 'kb': kb, 'vW': vW, 'vb': vb, 'oW': oW, 'ob': ob}
    _L0_xattn_all = _L0_xattn_setup()
    _L0_xattn_in = {k: v for k, v in _L0_xattn_all.items() if k in ('hW', 'hb', 'cW', 'cb', 'qW', 'qb', 'kW', 'kb', 'vW', 'vb', 'oW', 'ob')}
    del _L0_xattn_all

    def _L0_ffn_setup():
        import jax, jax.numpy as jnp
        import numpy as np
        E = 8
        D = 128
        F = 512
        S, B = (256, 2)
        LN_EPS = 1e-05

        def _moe_forward(input_features, centroids, ln_g, ln_b, W1, b1, W2, b2):
            s, b, d = input_features.shape
            x = jnp.swapaxes(input_features, 0, 1).reshape(-1, d)
            logits = x.astype(jnp.float32) @ centroids.astype(jnp.float32).T
            assign = jnp.argmax(logits, axis=-1)
            onehot = jax.nn.one_hot(assign, E, dtype=x.dtype)
            disp = jnp.einsum('te,td->etd', onehot, x)
            mu = disp.mean(-1, keepdims=True)
            var = disp.var(-1, keepdims=True)
            xn = (disp - mu) * jax.lax.rsqrt(var + LN_EPS)
            xn = xn * ln_g[:, None, :] + ln_b[:, None, :]
            h = jax.nn.relu(jnp.einsum('etd,edf->etf', xn, W1) + b1[:, None, :])
            y = jnp.einsum('etf,efd->etd', h, W2) + b2[:, None, :]
            y = disp + y
            out = jnp.einsum('te,etd->td', onehot, y)
            return jnp.swapaxes(out.reshape(b, s, d), 0, 1)
        key = jax.random.key(seed)
        ks = jax.random.split(key, 8)
        scale_in = 1.0 / np.sqrt(D)
        scale_ff = 1.0 / np.sqrt(F)
        return {'input_features': jax.random.normal(ks[0], (S, B, D), dtype=jnp.float32), 'centroids': jax.random.normal(ks[1], (E, D), dtype=jnp.float32) * scale_in, 'ln_g': jnp.ones((E, D), dtype=jnp.float32), 'ln_b': jnp.zeros((E, D), dtype=jnp.float32), 'W1': jax.random.normal(ks[2], (E, D, F), dtype=jnp.float32) * scale_in, 'b1': jax.random.normal(ks[3], (E, F), dtype=jnp.float32) * 0.01, 'W2': jax.random.normal(ks[4], (E, F, D), dtype=jnp.float32) * scale_ff, 'b2': jax.random.normal(ks[5], (E, D), dtype=jnp.float32) * 0.01}
    _L0_ffn_all = _L0_ffn_setup()
    _L0_ffn_in = {k: v for k, v in _L0_ffn_all.items() if k in ('centroids', 'ln_g', 'ln_b', 'W1', 'b1', 'W2', 'b2')}
    del _L0_ffn_all

    def _L1_attn_setup():
        import jax, jax.numpy as jnp
        import numpy as np
        NUM_HEAD = 16
        HEAD_DIM = 64
        RES_DIM = 128
        LN_EPS = 1e-05

        def _layer_norm(x, w, b):
            mu = jnp.mean(x, axis=-1, keepdims=True)
            var = jnp.var(x, axis=-1, keepdims=True)
            return (x - mu) * jax.lax.rsqrt(var + LN_EPS) * w + b
        key = jax.random.key(seed)
        k1, k2, k3 = jax.random.split(key, 3)
        slen, bsz = (256, 4)
        x = jax.random.normal(k1, (slen, bsz, RES_DIM), dtype=jnp.float32)
        w_qkv = jax.random.normal(k2, (NUM_HEAD * 3 * HEAD_DIM, RES_DIM), dtype=jnp.float32) * (1.0 / np.sqrt(RES_DIM))
        w_out = jax.random.normal(k3, (RES_DIM, NUM_HEAD * HEAD_DIM), dtype=jnp.float32) * (1.0 / np.sqrt(NUM_HEAD * HEAD_DIM))
        ln_w = jnp.ones((RES_DIM,), dtype=jnp.float32)
        ln_b = jnp.zeros((RES_DIM,), dtype=jnp.float32)
        return {'x': x, 'w_qkv': w_qkv, 'w_out': w_out, 'ln_w': ln_w, 'ln_b': ln_b}
    _L1_attn_all = _L1_attn_setup()
    _L1_attn_in = {k: v for k, v in _L1_attn_all.items() if k in ('w_qkv', 'w_out', 'ln_w', 'ln_b')}
    del _L1_attn_all

    def _L1_xattn_setup():
        import jax, jax.numpy as jnp
        import numpy as np
        D_MODEL = 128
        LOW_RANK = 128
        SCALE = 1.0 / np.sqrt(LOW_RANK)

        def _xavier(key, fan_out, fan_in):
            limit = np.sqrt(6.0 / (fan_in + fan_out))
            return jax.random.uniform(key, (fan_out, fan_in), jnp.float32, -limit, limit)
        key = jax.random.key(seed)
        k_tgt, k_mem, kq, kk, kv, ko = jax.random.split(key, 6)
        tgt = jax.random.normal(k_tgt, (4, 256, D_MODEL), jnp.float32)
        memory = jax.random.normal(k_mem, (4, 256, D_MODEL), jnp.float32)
        Wq = _xavier(kq, LOW_RANK, D_MODEL)
        Wk = _xavier(kk, LOW_RANK, D_MODEL)
        Wv = _xavier(kv, D_MODEL, D_MODEL)
        Wo = _xavier(ko, D_MODEL, D_MODEL)
        return {'tgt': tgt, 'memory': memory, 'Wq': Wq, 'Wk': Wk, 'Wv': Wv, 'Wo': Wo}
    _L1_xattn_all = _L1_xattn_setup()
    _L1_xattn_in = {k: v for k, v in _L1_xattn_all.items() if k in ('Wq', 'Wk', 'Wv', 'Wo')}
    del _L1_xattn_all

    def _L1_ffn_setup():
        import jax, jax.numpy as jnp
        import numpy as np
        DIM = 128
        DEPTH = 6
        HEADS = 16
        DIM_HEAD = 64
        WINDOW = 32
        INNER = HEADS * DIM_HEAD
        DIM_INNER = int(DIM * 4 * 2 / 3)
        QK_SCALE = 8.0

        def shift_tokens(t):
            a, s = jnp.split(t, 2, -1)
            s = jnp.pad(s, ((0, 0), (1, 0), (0, 0)))[:, :-1]
            return jnp.concatenate([a, s], -1)

        def l2norm(t):
            return t / jnp.maximum(jnp.linalg.norm(t, axis=-1, keepdims=True), 1e-12)

        def rotate_half(x):
            x1, x2 = jnp.split(x, 2, -1)
            return jnp.concatenate([-x2, x1], -1)

        def rotary_tables(n):
            half = jnp.arange(0, DIM_HEAD, 2, dtype=jnp.float32)
            inv_freq = 1.0 / 10000.0 ** (half / DIM_HEAD)
            t = jnp.arange(n, dtype=jnp.float32)
            freqs = t[:, None] * inv_freq[None, :]
            freqs = jnp.concatenate([freqs, freqs], -1)
            base_scale = (half + 0.4 * DIM_HEAD) / (1.4 * DIM_HEAD)
            power = (t - n // 2) / (WINDOW // 2)
            scale = base_scale[None, :] ** power[:, None]
            scale = jnp.concatenate([scale, scale], -1)
            return (freqs, scale)

        def local_attention(q, k, v):
            b, h, n, d = q.shape
            w = WINDOW
            nw = n // w
            bq = q.reshape(b, h, nw, w, d)
            bk = k.reshape(b, h, nw, w, d)
            bv = v.reshape(b, h, nw, w, d)

            def look(t):
                p = jnp.pad(t, ((0, 0), (0, 0), (1, 0), (0, 0), (0, 0)))
                return jnp.concatenate([p[:, :, :nw], p[:, :, 1:]], axis=3)
            bk2, bv2 = (look(bk), look(bv))
            seq = jnp.arange(n).reshape(nw, w)
            seq_p = jnp.pad(seq, ((1, 0), (0, 0)), constant_values=-1)
            jt = jnp.concatenate([seq_p[:nw], seq_p[1:]], axis=1)
            it = seq[:, :, None]
            jb = jt[:, None, :]
            mask = (it < jb) | (it > jb + w) | (jb == -1)
            sim = jnp.einsum('bhwie,bhwje->bhwij', bq, bk2) * QK_SCALE
            sim = jnp.where(mask, -jnp.finfo(sim.dtype).max, sim)
            attn = jax.nn.softmax(sim, -1)
            out = jnp.einsum('bhwij,bhwje->bhwie', attn, bv2)
            return out.reshape(b, h, n, d)

        def attn_layer(x, Wqkv, qs, ksc, Wo):
            b, n, _ = x.shape
            qkv = x @ Wqkv
            q, k, v = jnp.split(qkv, 3, -1)
            sh = lambda t: t.reshape(b, n, HEADS, DIM_HEAD).transpose(0, 2, 1, 3)
            q, k, v = (sh(q), sh(k), sh(v))
            q = l2norm(q) * qs
            k = l2norm(k) * ksc
            freqs, scale = rotary_tables(n)
            cos, sin = (jnp.cos(freqs), jnp.sin(freqs))
            q = q * cos * scale + rotate_half(q) * sin * scale
            inv = 1.0 / scale
            k = k * cos * inv + rotate_half(k) * sin * inv
            out = local_attention(q, k, v)
            out = out.transpose(0, 2, 1, 3).reshape(b, n, INNER)
            return out @ Wo

        def ffn_layer(x, g, bln, W1, b1, W2, b2):
            mu = x.mean(-1, keepdims=True)
            var = ((x - mu) ** 2).mean(-1, keepdims=True)
            xn = (x - mu) / jnp.sqrt(var + 1e-05) * g + bln
            hg = xn @ W1 + b1
            a, gate = jnp.split(hg, 2, -1)
            return a * jax.nn.gelu(gate, approximate=False) @ W2 + b2
        key = jax.random.key(seed)
        ks = jax.random.split(key, 8)
        B, N = (2, 256)
        init = lambda k, shape: jax.random.normal(k, shape, jnp.float32) * 0.02
        return {'x': jax.random.normal(ks[0], (B, N, DIM), jnp.float32), 'Wqkv': init(ks[1], (DEPTH, DIM, 3 * INNER)), 'q_scale': jnp.ones((DEPTH, DIM_HEAD), jnp.float32), 'k_scale': jnp.ones((DEPTH, DIM_HEAD), jnp.float32), 'Wo': init(ks[2], (DEPTH, INNER, DIM)), 'ln_g': jnp.ones((DEPTH, DIM), jnp.float32), 'ln_b': jnp.zeros((DEPTH, DIM), jnp.float32), 'W1': init(ks[3], (DEPTH, DIM, 2 * DIM_INNER)), 'b1': jnp.zeros((DEPTH, 2 * DIM_INNER), jnp.float32), 'W2': init(ks[4], (DEPTH, DIM_INNER, DIM)), 'b2': jnp.zeros((DEPTH, DIM), jnp.float32)}
    _L1_ffn_all = _L1_ffn_setup()
    _L1_ffn_in = {k: v for k, v in _L1_ffn_all.items() if k in ('Wqkv', 'q_scale', 'k_scale', 'Wo', 'ln_g', 'ln_b', 'W1', 'b1', 'W2', 'b2')}
    del _L1_ffn_all
    return {'x': x, 'ctx_1024': ctx_1024, 'L0_attn_Wq': _L0_attn_in['Wq'], 'L0_attn_bq': _L0_attn_in['bq'], 'L0_attn_Wk': _L0_attn_in['Wk'], 'L0_attn_bk': _L0_attn_in['bk'], 'L0_attn_Wv': _L0_attn_in['Wv'], 'L0_attn_bv': _L0_attn_in['bv'], 'L0_attn_rel_emb': _L0_attn_in['rel_emb'], 'L0_xattn_hW': _L0_xattn_in['hW'], 'L0_xattn_hb': _L0_xattn_in['hb'], 'L0_xattn_cW': _L0_xattn_in['cW'], 'L0_xattn_cb': _L0_xattn_in['cb'], 'L0_xattn_qW': _L0_xattn_in['qW'], 'L0_xattn_qb': _L0_xattn_in['qb'], 'L0_xattn_kW': _L0_xattn_in['kW'], 'L0_xattn_kb': _L0_xattn_in['kb'], 'L0_xattn_vW': _L0_xattn_in['vW'], 'L0_xattn_vb': _L0_xattn_in['vb'], 'L0_xattn_oW': _L0_xattn_in['oW'], 'L0_xattn_ob': _L0_xattn_in['ob'], 'L0_ffn_centroids': _L0_ffn_in['centroids'], 'L0_ffn_ln_g': _L0_ffn_in['ln_g'], 'L0_ffn_ln_b': _L0_ffn_in['ln_b'], 'L0_ffn_W1': _L0_ffn_in['W1'], 'L0_ffn_b1': _L0_ffn_in['b1'], 'L0_ffn_W2': _L0_ffn_in['W2'], 'L0_ffn_b2': _L0_ffn_in['b2'], 'L1_attn_w_qkv': _L1_attn_in['w_qkv'], 'L1_attn_w_out': _L1_attn_in['w_out'], 'L1_attn_ln_w': _L1_attn_in['ln_w'], 'L1_attn_ln_b': _L1_attn_in['ln_b'], 'L1_xattn_Wq': _L1_xattn_in['Wq'], 'L1_xattn_Wk': _L1_xattn_in['Wk'], 'L1_xattn_Wv': _L1_xattn_in['Wv'], 'L1_xattn_Wo': _L1_xattn_in['Wo'], 'L1_ffn_Wqkv': _L1_ffn_in['Wqkv'], 'L1_ffn_q_scale': _L1_ffn_in['q_scale'], 'L1_ffn_k_scale': _L1_ffn_in['k_scale'], 'L1_ffn_Wo': _L1_ffn_in['Wo'], 'L1_ffn_ln_g': _L1_ffn_in['ln_g'], 'L1_ffn_ln_b': _L1_ffn_in['ln_b'], 'L1_ffn_W1': _L1_ffn_in['W1'], 'L1_ffn_b1': _L1_ffn_in['b1'], 'L1_ffn_W2': _L1_ffn_in['W2'], 'L1_ffn_b2': _L1_ffn_in['b2']}

def reference(x, ctx_1024, L0_attn_Wq, L0_attn_bq, L0_attn_Wk, L0_attn_bk, L0_attn_Wv, L0_attn_bv, L0_attn_rel_emb, L0_xattn_hW, L0_xattn_hb, L0_xattn_cW, L0_xattn_cb, L0_xattn_qW, L0_xattn_qb, L0_xattn_kW, L0_xattn_kb, L0_xattn_vW, L0_xattn_vb, L0_xattn_oW, L0_xattn_ob, L0_ffn_centroids, L0_ffn_ln_g, L0_ffn_ln_b, L0_ffn_W1, L0_ffn_b1, L0_ffn_W2, L0_ffn_b2, L1_attn_w_qkv, L1_attn_w_out, L1_attn_ln_w, L1_attn_ln_b, L1_xattn_Wq, L1_xattn_Wk, L1_xattn_Wv, L1_xattn_Wo, L1_ffn_Wqkv, L1_ffn_q_scale, L1_ffn_k_scale, L1_ffn_Wo, L1_ffn_ln_g, L1_ffn_ln_b, L1_ffn_W1, L1_ffn_b1, L1_ffn_W2, L1_ffn_b2):
    import jax
    import jax.numpy as jnp

    def _L0_attn_ref(x, Wq, bq, Wk, bk, Wv, bv, rel_emb):
        import jax, jax.numpy as jnp
        import numpy as np
        D_MODEL = 128
        NUM_HEADS = 16
        MAX_LEN = 256
        BATCH = 2
        SEQ_LEN = 256
        B, L, D = x.shape
        H = rel_emb.shape[0]
        dk = D // H

        def heads(y):
            return y.reshape(B, L, H, dk).transpose(0, 2, 1, 3)
        q = heads(x @ Wq + bq)
        k = heads(x @ Wk + bk)
        v = heads(x @ Wv + bv)
        scores = jnp.einsum('bhid,bhjd->bhij', q, k) / jnp.sqrt(jnp.float32(dk))
        pos = jnp.arange(L)
        rel_idx = pos[:, None] - pos[None, :] + (L - 1)
        bias = rel_emb[:, rel_idx]
        attn = jax.nn.softmax(scores + bias[None], axis=-1)
        out = jnp.einsum('bhij,bhjd->bhid', attn, v)
        return out.transpose(0, 2, 1, 3).reshape(B, L, D)

    def _L0_xattn_ref(history_features, combined_features, hW, hb, cW, cb, qW, qb, kW, kb, vW, vb, oW, ob):
        import jax, jax.numpy as jnp
        import numpy as np
        B, LQ, LK = (8, 256, 256)
        HIST_DIM, COMB_DIM, FUSION_DIM = (128, 128, 128)

        def _linear_params(key, in_dim, out_dim):
            k1, k2 = jax.random.split(key)
            bound = 1.0 / np.sqrt(in_dim)
            W = jax.random.uniform(k1, (out_dim, in_dim), jnp.float32, -bound, bound)
            b = jax.random.uniform(k2, (out_dim,), jnp.float32, -bound, bound)
            return (W, b)

        def _lin(x, W, b):
            return jnp.einsum('bld,fd->blf', x, W) + b
        h = _lin(history_features, hW, hb)
        c = _lin(combined_features, cW, cb)
        q = _lin(h, qW, qb)
        k = _lin(c, kW, kb)
        v = _lin(c, vW, vb)
        scale = 1.0 / jnp.sqrt(jnp.float32(FUSION_DIM))
        scores = jnp.einsum('bqf,bkf->bqk', q, k) * scale
        attn = jax.nn.softmax(scores, axis=-1)
        attn_out = jnp.einsum('bqk,bkf->bqf', attn, v)
        return _lin(attn_out + q, oW, ob)

    def _L0_ffn_ref(input_features, centroids, ln_g, ln_b, W1, b1, W2, b2):
        import jax, jax.numpy as jnp
        import numpy as np
        E = 8
        D = 128
        F = 512
        S, B = (256, 2)
        LN_EPS = 1e-05

        def _moe_forward(input_features, centroids, ln_g, ln_b, W1, b1, W2, b2):
            s, b, d = input_features.shape
            x = jnp.swapaxes(input_features, 0, 1).reshape(-1, d)
            logits = x.astype(jnp.float32) @ centroids.astype(jnp.float32).T
            assign = jnp.argmax(logits, axis=-1)
            onehot = jax.nn.one_hot(assign, E, dtype=x.dtype)
            disp = jnp.einsum('te,td->etd', onehot, x)
            mu = disp.mean(-1, keepdims=True)
            var = disp.var(-1, keepdims=True)
            xn = (disp - mu) * jax.lax.rsqrt(var + LN_EPS)
            xn = xn * ln_g[:, None, :] + ln_b[:, None, :]
            h = jax.nn.relu(jnp.einsum('etd,edf->etf', xn, W1) + b1[:, None, :])
            y = jnp.einsum('etf,efd->etd', h, W2) + b2[:, None, :]
            y = disp + y
            out = jnp.einsum('te,etd->td', onehot, y)
            return jnp.swapaxes(out.reshape(b, s, d), 0, 1)
        return _moe_forward(input_features, centroids, ln_g, ln_b, W1, b1, W2, b2)

    def _L1_attn_ref(x, w_qkv, w_out, ln_w, ln_b):
        import jax, jax.numpy as jnp
        import numpy as np
        NUM_HEAD = 16
        HEAD_DIM = 64
        RES_DIM = 128
        LN_EPS = 1e-05

        def _layer_norm(x, w, b):
            mu = jnp.mean(x, axis=-1, keepdims=True)
            var = jnp.var(x, axis=-1, keepdims=True)
            return (x - mu) * jax.lax.rsqrt(var + LN_EPS) * w + b
        slen, bsz, _ = x.shape
        scale = 1.0 / np.sqrt(RES_DIM).astype(np.float32)
        x_in = _layer_norm(x, ln_w, ln_b)
        qkv = x_in @ w_qkv.T
        qkv = qkv.reshape(slen, bsz, NUM_HEAD, 3 * HEAD_DIM)
        q, k, v = jnp.split(qkv, 3, axis=-1)
        scores = jnp.einsum('ibnd,jbnd->ijbn', q, k) * scale
        attn = jax.nn.softmax(scores, axis=1)
        attn_out = jnp.einsum('ijbn,jbnd->ibnd', attn, v)
        attn_out = attn_out.reshape(slen, bsz, NUM_HEAD * HEAD_DIM)
        attn_out = attn_out @ w_out.T
        return x + attn_out

    def _L1_xattn_ref(tgt, memory, Wq, Wk, Wv, Wo):
        import jax, jax.numpy as jnp
        import numpy as np
        D_MODEL = 128
        LOW_RANK = 128
        SCALE = 1.0 / np.sqrt(LOW_RANK)

        def _xavier(key, fan_out, fan_in):
            limit = np.sqrt(6.0 / (fan_in + fan_out))
            return jax.random.uniform(key, (fan_out, fan_in), jnp.float32, -limit, limit)
        q = jnp.einsum('btd,rd->btr', tgt, Wq)
        k = jnp.einsum('bsd,rd->bsr', memory, Wk)
        v = jnp.einsum('bsd,ed->bse', memory, Wv)
        scores = jnp.einsum('btr,bsr->bts', q, k) * SCALE
        attn = jax.nn.softmax(scores, axis=-1)
        attn_out = jnp.einsum('bts,bse->bte', attn, v)
        return jnp.einsum('bte,oe->bto', attn_out, Wo)

    def _L1_ffn_ref(x, Wqkv, q_scale, k_scale, Wo, ln_g, ln_b, W1, b1, W2, b2):
        import jax, jax.numpy as jnp
        import numpy as np
        DIM = 128
        DEPTH = 6
        HEADS = 16
        DIM_HEAD = 64
        WINDOW = 32
        INNER = HEADS * DIM_HEAD
        DIM_INNER = int(DIM * 4 * 2 / 3)
        QK_SCALE = 8.0

        def shift_tokens(t):
            a, s = jnp.split(t, 2, -1)
            s = jnp.pad(s, ((0, 0), (1, 0), (0, 0)))[:, :-1]
            return jnp.concatenate([a, s], -1)

        def l2norm(t):
            return t / jnp.maximum(jnp.linalg.norm(t, axis=-1, keepdims=True), 1e-12)

        def rotate_half(x):
            x1, x2 = jnp.split(x, 2, -1)
            return jnp.concatenate([-x2, x1], -1)

        def rotary_tables(n):
            half = jnp.arange(0, DIM_HEAD, 2, dtype=jnp.float32)
            inv_freq = 1.0 / 10000.0 ** (half / DIM_HEAD)
            t = jnp.arange(n, dtype=jnp.float32)
            freqs = t[:, None] * inv_freq[None, :]
            freqs = jnp.concatenate([freqs, freqs], -1)
            base_scale = (half + 0.4 * DIM_HEAD) / (1.4 * DIM_HEAD)
            power = (t - n // 2) / (WINDOW // 2)
            scale = base_scale[None, :] ** power[:, None]
            scale = jnp.concatenate([scale, scale], -1)
            return (freqs, scale)

        def local_attention(q, k, v):
            b, h, n, d = q.shape
            w = WINDOW
            nw = n // w
            bq = q.reshape(b, h, nw, w, d)
            bk = k.reshape(b, h, nw, w, d)
            bv = v.reshape(b, h, nw, w, d)

            def look(t):
                p = jnp.pad(t, ((0, 0), (0, 0), (1, 0), (0, 0), (0, 0)))
                return jnp.concatenate([p[:, :, :nw], p[:, :, 1:]], axis=3)
            bk2, bv2 = (look(bk), look(bv))
            seq = jnp.arange(n).reshape(nw, w)
            seq_p = jnp.pad(seq, ((1, 0), (0, 0)), constant_values=-1)
            jt = jnp.concatenate([seq_p[:nw], seq_p[1:]], axis=1)
            it = seq[:, :, None]
            jb = jt[:, None, :]
            mask = (it < jb) | (it > jb + w) | (jb == -1)
            sim = jnp.einsum('bhwie,bhwje->bhwij', bq, bk2) * QK_SCALE
            sim = jnp.where(mask, -jnp.finfo(sim.dtype).max, sim)
            attn = jax.nn.softmax(sim, -1)
            out = jnp.einsum('bhwij,bhwje->bhwie', attn, bv2)
            return out.reshape(b, h, n, d)

        def attn_layer(x, Wqkv, qs, ksc, Wo):
            b, n, _ = x.shape
            qkv = x @ Wqkv
            q, k, v = jnp.split(qkv, 3, -1)
            sh = lambda t: t.reshape(b, n, HEADS, DIM_HEAD).transpose(0, 2, 1, 3)
            q, k, v = (sh(q), sh(k), sh(v))
            q = l2norm(q) * qs
            k = l2norm(k) * ksc
            freqs, scale = rotary_tables(n)
            cos, sin = (jnp.cos(freqs), jnp.sin(freqs))
            q = q * cos * scale + rotate_half(q) * sin * scale
            inv = 1.0 / scale
            k = k * cos * inv + rotate_half(k) * sin * inv
            out = local_attention(q, k, v)
            out = out.transpose(0, 2, 1, 3).reshape(b, n, INNER)
            return out @ Wo

        def ffn_layer(x, g, bln, W1, b1, W2, b2):
            mu = x.mean(-1, keepdims=True)
            var = ((x - mu) ** 2).mean(-1, keepdims=True)
            xn = (x - mu) / jnp.sqrt(var + 1e-05) * g + bln
            hg = xn @ W1 + b1
            a, gate = jnp.split(hg, 2, -1)
            return a * jax.nn.gelu(gate, approximate=False) @ W2 + b2
        for i in range(DEPTH):
            x = attn_layer(shift_tokens(x), Wqkv[i], q_scale[i], k_scale[i], Wo[i]) + x
            x = ffn_layer(shift_tokens(x), ln_g[i], ln_b[i], W1[i], b1[i], W2[i], b2[i]) + x
        return x
    x = x + _L0_attn_ref(_layernorm(x, axis=-1), L0_attn_Wq, L0_attn_bq, L0_attn_Wk, L0_attn_bk, L0_attn_Wv, L0_attn_bv, L0_attn_rel_emb)
    x = x + _L0_xattn_ref(_layernorm(x, axis=-1), ctx_1024, L0_xattn_hW, L0_xattn_hb, L0_xattn_cW, L0_xattn_cb, L0_xattn_qW, L0_xattn_qb, L0_xattn_kW, L0_xattn_kb, L0_xattn_vW, L0_xattn_vb, L0_xattn_oW, L0_xattn_ob)
    x = x + _L0_ffn_ref(_layernorm(x, axis=-1), L0_ffn_centroids, L0_ffn_ln_g, L0_ffn_ln_b, L0_ffn_W1, L0_ffn_b1, L0_ffn_W2, L0_ffn_b2)
    x = x + _L1_attn_ref(_layernorm(x, axis=-1), L1_attn_w_qkv, L1_attn_w_out, L1_attn_ln_w, L1_attn_ln_b)
    x = x + _L1_xattn_ref(_layernorm(x, axis=-1), ctx_1024, L1_xattn_Wq, L1_xattn_Wk, L1_xattn_Wv, L1_xattn_Wo)
    x = x + _L1_ffn_ref(_layernorm(x, axis=-1), L1_ffn_Wqkv, L1_ffn_q_scale, L1_ffn_k_scale, L1_ffn_Wo, L1_ffn_ln_g, L1_ffn_ln_b, L1_ffn_W1, L1_ffn_b1, L1_ffn_W2, L1_ffn_b2)
    return x

_drawn_inputs = setup_inputs


def setup_inputs(seed=0):
    import zlib

    import numpy as np

    out = dict(_drawn_inputs(seed))
    spreads = {'L0_attn_bq': (0.0, 0.8),
     'L0_attn_bk': (0.0, 2.0),
     'L0_attn_bv': (0.0, 0.1),
     'L0_ffn_ln_g': (1.0, 0.2),
     'L0_ffn_ln_b': (0.0, 0.1),
     'L1_attn_ln_w': (1.0, 0.2),
     'L1_attn_ln_b': (0.0, 0.269),
     'L1_ffn_q_scale': (1.0, 0.6),
     'L1_ffn_k_scale': (1.0, 0.6),
     'L1_ffn_ln_g': (1.0, 0.6),
     'L1_ffn_ln_b': (0.0, 0.8),
     'L1_ffn_b1': (0.0, 0.8),
     'L1_ffn_b2': (0.0, 0.641)}
    factors = {'L0_attn_Wq': 3.872,
     'L0_attn_Wk': 4.353,
     'L0_xattn_kW': 3.913,
     'L0_xattn_kb': 64.0,
     'L0_ffn_b1': 8.0,
     'L0_ffn_b2': 8.0,
     'L1_ffn_W1': 7.716,
     'L1_ffn_W2': 7.611}
    for name, (base, spread) in spreads.items():
        noise = np.random.default_rng([zlib.crc32(name.encode()), seed]).standard_normal(out[name].shape)
        drawn = base * np.exp(spread * noise) if base else spread * noise
        out[name] = jnp.asarray(drawn.astype(out[name].dtype))
    for name, factor in factors.items():
        out[name] = (out[name] * factor).astype(out[name].dtype)
    return out
```

```python
from contextlib import ExitStack

import concourse.bass as bass
from concourse import mybir

F32 = mybir.dt.float32
BF16 = mybir.dt.bfloat16
ACT = mybir.ActivationFunctionType
ALU = mybir.AluOpType
AXX = mybir.AxisListType.X

P = 128
T = 1024
HC = 512
NB = 4
SEQ = 256
EPS = 1e-5
BIG = 3.0e38

AH, ADK = 16, 8
SK = 1601
KT = (SK + P - 1) // P
KLAST = SK - (KT - 1) * P
XSCALE = 1.0 / float(P) ** 0.5
NE, FF = 8, 512
FT = FF // P
NH, DH = 16, 64
CH = NH * DH // P
DEPTH, WIN = 6, 32
GI = 341
GT = 3
QK_SCALE = 8.0
SEGF = P + WIN

V_BQ, V_BK, V_BV, V_HB, V_QB, V_KB, V_CB, V_VB, V_OB, V_LW, V_LB = range(11)
V_EG, V_EB, V_EB2, V_EB1 = 11, 19, 27, 35
NVEC = V_EB1 + NE * FT
L_G, L_B, L_B2, L_B1A, L_B1G = 0, 1, 2, 3, 6
NLV = 9
C_ID, C_MEAN, C_BLK, C_HM, C_PR, C_MD, C_MF, C_ROT = 0, 128, 256, 384, 400, 432, 560, 880
NCST = C_ROT + 4 * 2 * DH


def ln_steps(name, exact):
    return [f"{name}.{s}" for s in ["mean", "xc", "sq", "var", "rs"] + ["rc"] * exact + ["out"]]


def pairs(name, what):
    return [f"{name}.{w}{e}" for w in what for e in ("", "e")]


CHAIN = (ln_steps("A", True) + pairs("A", "qkv") + [f"A.{w}{j}" for j in range(2) for w in ("rc", "on", "ot", "res")]
         + ln_steps("B", True) + pairs("B", "hquws") + ["B.core"] + pairs("B", "cvo")
         + ln_steps("C", True) + ln_steps("C2", False) + ["C.addx"]
         + ["C.lg", "C.mx", "C.eq", "C.pr", "C.m2", "C.oh"] + [f"C.{w}{e}" for e in range(NE) for w in ("bc", "be")]
         + ["C.core"]
         + ln_steps("D", False) + ln_steps("D2", False) + ["D.addx", "D.aff"]
         + ln_steps("E", False) + pairs("E", "qw") + ["E.core"] + pairs("E", "vo")
         + ln_steps("F", False))
AT = {n: i for i, n in enumerate(CHAIN)}
LAYER = (["shift", "v", "core", "wo", "woe", "shift2"] + ln_steps("f", False) + ["aff", "ffn", "w2", "w2e"])
LAT = {n: i for i, n in enumerate(LAYER)}


def decoder(nc, xT, cst, vec, wa, rel, ctxT, ctxN, wb, cen, we1, we2, wd, we, lvec, wfq, scl, wfo, wf1, wf2, out):
    with ExitStack() as ctx:
        def sb(name, cols, dt=F32):
            return ctx.enter_context(nc.sbuf_tensor(name, [P, cols], dt))

        def sem(name):
            return ctx.enter_context(nc.semaphore(name))

        X, XC, SQ, RS, XN, XI = (sb(n, T) for n in ("X", "XC", "SQ", "RS", "XN", "XI"))
        CST = sb("CST", NCST)
        VEC = sb("VEC", NVEC)
        LV = sb("LV", NLV)
        LV6 = sb("LV6", DEPTH * NLV)
        IDB = sb("IDB", P, BF16)
        MDB = sb("MDB", P, BF16)
        MFB = sb("MFB", 2 * SEGF, BF16)
        small = sb("small", 256)
        W_A = sb("W_A", 3 * P)
        W_B = sb("W_B", 7 * P)
        W_E = sb("W_E", 4 * P)
        CEN = sb("CEN", NE)
        MOE = sb("MOE", 2 * NE * FF)
        REL = sb("REL", AH * 3 * P)
        WORK = sb("WORK", 13060 + 11600)

        ident = CST[:, C_ID:C_ID + P]
        mean_w = CST[:, C_MEAN:C_MEAN + P]
        block_w = CST[:, C_BLK:C_BLK + P]
        head_mask = CST[:, C_HM:C_HM + AH]
        prio = CST[:, C_PR:C_PR + 4 * NE].rearrange("p (a e) -> p a e", e=NE)

        def carve(at, cols):
            return WORK[:, at:at + cols], at + cols

        o = 0
        CT, o = carve(o, NB * SK)
        CN, o = carve(o, NB * KT * P)
        ctx_end = o
        CT3 = CT.rearrange("p (b k) -> p b k", b=NB)
        CN4 = CN.rearrange("p (b j d) -> p b j d", b=NB, d=P)
        rel3 = REL[:, :].rearrange("p (h c) -> p h c", h=AH)
        a = ctx_end
        KM, a = carve(a, 2 * AH * SEQ)
        KM4 = KM.rearrange("p (n h k) -> p n h k", n=2, h=AH)
        NS, a = carve(a, 2 * 512)
        PA, a = carve(a, 2 * 512)
        PTA, a = carve(a, 2 * 512)
        NS4 = NS.rearrange("p (n i k) -> p n i k", n=2, i=2)
        PA4 = PA.rearrange("p (n i k) -> p n i k", n=2, i=2)
        PTA4 = PTA.rearrange("p (n j q) -> p n j q", n=2, j=4)
        assert a <= 13060 + 11600
        QA, KA, VA = XI[:, :], SQ[:, :], RS[:, :]
        VA3 = VA.rearrange("p (t d) -> p t d", d=P)
        ON_A = XC[:, 0:512].rearrange("p (n q m) -> p n q m", n=2, q=2)
        a = ctx_end
        XQ, a = carve(a, T)
        XU, a = carve(a, T)
        XW, a = carve(a, T)
        XA, a = carve(a, T)
        PX, a = carve(a, 2 * SK)
        PX3 = PX.rearrange("p (n k) -> p n k", n=2)
        PTX, a = carve(a, 2 * KT * P)
        PTX4 = PTX.rearrange("p (n j q) -> p n j q", n=2, q=P)
        ONX, a = carve(a, 2 * P)
        ONX3 = ONX.rearrange("p (n d) -> p n d", n=2)
        assert a <= 13060 + 11600
        W1M = MOE[:, 0:NE * FF].rearrange("p (e f) -> p e f", e=NE)
        W2M = MOE[:, NE * FF:2 * NE * FF].rearrange("p (e j d) -> p e j d", e=NE, d=P)
        a = ctx_end
        HM, a = carve(a, 2 * FT * HC)
        HM4 = HM.rearrange("p (n j t) -> p n j t", n=2, j=FT)
        XE, a = carve(a, 2 * HC)
        XE3 = XE.rearrange("p (n t) -> p n t", n=2)
        YE, a = carve(a, 2 * HC)
        YE3 = YE.rearrange("p (n t) -> p n t", n=2)
        OHW, a = carve(a, NE * T // 2)
        OH = OHW.bitcast(BF16).rearrange("p (e t) -> p e t", e=NE)
        assert a <= 13060 + 11600
        OHT = small[:, 192:224].bitcast(BF16).rearrange("p (h a e) -> p h a e", h=2, e=NE)
        WDQ = REL[:, 0:3 * NH * DH]
        WDO = REL[:, 3 * NH * DH:3 * NH * DH + CH * P].rearrange("p (c d) -> p c d", c=CH)
        a = ctx_end
        QD, a = carve(a, CH * 256)
        KD, a = carve(a, CH * 256)
        VD, a = carve(a, 4 * NH * (DH + 1))
        OD, a = carve(a, 2 * NH * DH)
        XD, a = carve(a, T)
        XD4 = XD.rearrange("p (n i b) -> p n i b", n=8, i=4)
        assert a <= 13060 + 11600
        QD3, KD3 = (z.rearrange("p (c t) -> p c t", c=CH) for z in (QD, KD))
        VD4 = VD.rearrange("p (n h k) -> p n h k", n=4, k=DH + 1)
        OD3 = OD.rearrange("p (n m) -> p n m", n=2)
        PD4 = SQ[:, :].rearrange("p (n i k) -> p n i k", n=2, i=4)
        PTD4 = XC[:, :].rearrange("p (n i q) -> p n i q", n=2, i=4)
        OTD3 = RS[:, :].rearrange("p (c q) -> p c q", c=CH)
        a = 0
        VF, a = carve(a, 4 * NH * (DH + 1))
        KN, a = carve(a, 4 * NH * DH)
        QN, a = carve(a, 4 * NH * DH)
        QTF, a = carve(a, 2 * SEQ)
        KPF, a = carve(a, 2 * 2 * (SEQ + WIN))
        XSF, a = carve(a, T)
        SQF, a = carve(a, 2 * HC)
        T2F, a = carve(a, 2 * HC)
        PF, a = carve(a, 3 * 512)
        PTF, a = carve(a, 2 * 384)
        GF, a = carve(a, GT * HC)
        YF, a = carve(a, T)
        assert a <= 13060 + 11600, a
        OTF = REL[:, 0:CH * HC].rearrange("p (c t) -> p c t", c=CH)
        ONF = REL[:, CH * HC:CH * HC + 2 * 2 * P].rearrange("p (n q m) -> p n q m", n=2, q=2)
        HF3 = REL[:, CH * HC + 4 * P:CH * HC + 4 * P + GT * HC].rearrange("p (n t) -> p n t", n=GT)
        VF4 = VF.rearrange("p (n h k) -> p n h k", n=4, k=DH + 1)
        KN3, QN3 = (z.rearrange("p (n m) -> p n m", n=4) for z in (KN, QN))
        QTF3 = QTF.rearrange("p (n t) -> p n t", n=2)
        KPF4 = KPF.rearrange("p (n r t) -> p n r t", n=2, r=2)
        SQF3, T2F3 = (z.rearrange("p (n t) -> p n t", n=2) for z in (SQF, T2F))
        PF3 = PF.rearrange("p (n k) -> p n k", n=3)
        PTF4 = PTF.rearrange("p (n j q) -> p n j q", n=2, j=3)
        GF3 = GF.rearrange("p (n t) -> p n t", n=GT)
        TABF = XN[:, 0:512].rearrange("p (n q d) -> p n q d", n=4, q=2)
        NSQ, NRM, NRC = (XN[:, 512 + 128 * z:640 + 128 * z].rearrange("p (w n h) -> p w n h", w=2, n=4) for z in range(3))
        WFQ = MOE[:, 0:3072]
        WFO = MOE[:, 5120:6144].rearrange("p (c d) -> p c d", c=CH)
        WF1 = MOE[:, 6144:6144 + 2 * GI]
        WF2 = MOE[:, 6144 + 2 * GI:6144 + 2 * GI + GT * P].rearrange("p (j d) -> p j d", j=GT)
        LQ6 = MOE[:, 3072:3072 + DEPTH * 4 * DH]

        PS = [ctx.enter_context(nc.psum_tensor(f"ps{i}", [P, 512], F32)) for i in range(2)]
        PQ = ctx.enter_context(nc.psum_tensor("pq", [P, 4, 512], F32))
        PR = [ctx.enter_context(nc.psum_tensor(f"pr{i}", [P, 512], F32)) for i in range(2)]

        half = [sem("half0"), sem("half1")]
        ld_x, ld_c, ld_v, ld_a, ld_rel, ld_ct, ld_cn, ld_b, ld_moe, ld_d, ld_e = (
            sem(f"ld_{n}") for n in "x cst vec a rel ct cn b moe d e".split())
        cast = sem("cast")
        a_km, a_s, a_ns, a_e, a_t, a_pt, a_o = (sem(f"a_{n}") for n in "km s ns e t pt o".split())
        x_s, x_mx, x_nb1, x_nb2, x_e, x_t, x_pta, x_ptd, x_o, x_rc, x_on, x_ot, x_at = (
            sem(f"x_{n}") for n in "s mx nb1 nb2 e t pta ptd o rc on ot at".split())
        c_xe, c_h, c_r, c_y, c_ye, c_acc = (sem(f"c_{n}") for n in "xe h r y ye acc".split())
        d_p, d_va, d_vd, d_s, d_mx, d_sub, d_e, d_t, d_pt, d_o, d_rc, d_on, d_wo, d_res, d_one = (
            sem(f"d_{n}") for n in "p va vd s mx sub e t pt o rc on wo res one".split())
        f_lv, f_tab, f_qp, f_sq, f_red, f_nrm, f_gd, f_rc1, f_t2, f_t1, f_add, f_km, f_v, f_va, f_vd, f_qt, f_ke = (
            sem(f"f_{n}") for n in "lv tab qp sq red nrm gd rc1 t2 t1 add km v va vd qt ke".split())
        f_s, f_mx, f_sub, f_e, f_t, f_pt, f_o, f_rc, f_on, f_g, f_a, f_ge, f_hh = (
            sem(f"f_{n}") for n in "s mx sub e t pt o rc on g a ge hh".split())
        ld_lv, ld_fq, ld_fo, ld_f1 = (sem(f"ld_{n}") for n in "lv fq fo f1".split())
        stored = sem("stored")

        d_jobs = []
        for u in range(32 + 3):
            d_jobs += [("p", u - 1)] * (1 <= u <= 32) + [("o", u // 4 - 1, g) for g in range(2) if u >= 6 and (u - 3) % 4 == 3]
        d_job = {j: n for n, j in enumerate(d_jobs)}
        f_jobs = []
        for u in range(32 + 4):
            f_jobs += [("p", u - 2)] * (2 <= u <= 33) + [("o", (u - 4) // 2)] * (u >= 5 and u % 2 == 1)
        f_job = {j: n for n, j in enumerate(f_jobs)}

        block = ctx.enter_context(nc.Block())
        HALVES = range(2)

        def cols(h):
            return slice(h * HC, (h + 1) * HC)

        def at(t, h):
            return t[:, cols(h)] if t.shape[1] == T else t[:, :]

        def turn(eng, h, name):
            if AT[name]:
                eng.wait_ge(half[h], AT[name])

        def ln_pe(pe, name, src, halves=HALVES, turn=turn):
            for h in halves:
                turn(pe, h, f"{name}.mean")
                nc.tensor.matmul(PS[h][:, :], mean_w, at(src, h), start=True, stop=True).then_inc(half[h], 1)
            for h in halves:
                turn(pe, h, f"{name}.var")
                nc.tensor.matmul(PS[h][:, :], mean_w, SQ[:, cols(h)], start=True, stop=True).then_inc(half[h], 1)

        def ln_act(act, name, exact, halves=HALVES, turn=turn):
            for h in halves:
                turn(act, h, f"{name}.sq")
                nc.scalar.activation(SQ[:, cols(h)], XC[:, cols(h)], ACT.Square).then_inc(half[h], 1)
            for h in halves:
                turn(act, h, f"{name}.rs")
                nc.scalar.activation(RS[:, cols(h)], PS[h][:, :], ACT.Sqrt if exact else ACT.Abs_reciprocal_sqrt,
                                     bias=eps_ap).then_inc(half[h], 1)

        def ln_dve(dve, name, src, dst, exact, halves=HALVES, turn=turn):
            for h in halves:
                turn(dve, h, f"{name}.xc")
                nc.vector.tensor_tensor(XC[:, cols(h)], at(src, h), PS[h][:, :], ALU.subtract).then_inc(half[h], 1)
            for h in halves:
                if exact:
                    turn(dve, h, f"{name}.rc")
                    nc.vector.reciprocal(RS[:, cols(h)], RS[:, cols(h)]).then_inc(half[h], 1)
            for h in halves:
                turn(dve, h, f"{name}.out")
                nc.vector.tensor_tensor(at(dst, h), XC[:, cols(h)], RS[:, cols(h)], ALU.mult).then_inc(half[h], 1)

        eps_ap = small[:, 255:256]

        def proj_pe(pe, name, w, src):
            for h in HALVES:
                turn(pe, h, name)
                nc.tensor.matmul(PS[h][:, :], w, src[:, cols(h)], start=True, stop=True).then_inc(half[h], 1)

        def bias_act(act, name, dst, col):
            for h in HALVES:
                turn(act, h, name)
                if col is None:
                    ins = nc.scalar.activation(dst[:, cols(h)], PS[h][:, :], ACT.Copy)
                else:
                    ins = nc.scalar.activation(dst[:, cols(h)], PS[h][:, :], ACT.Identity, bias=VEC[:, col:col + 1])
                ins.then_inc(half[h], 1)

        def add_dve(dve, name, dst, col, other):
            for h in HALVES:
                turn(dve, h, name)
                if col is None:
                    ins = nc.vector.tensor_tensor(dst[:, cols(h)], PS[h][:, :], other[:, cols(h)], ALU.add)
                else:
                    ins = nc.vector.scalar_tensor_tensor(dst[:, cols(h)], PS[h][:, :], VEC[:, col:col + 1],
                                                         other[:, cols(h)], ALU.add, ALU.add)
                ins.then_inc(half[h], 1)

        def x_pe(pe, k, W):
            name = ("B", "E")[k]

            def scores(t):
                b, h = t // 2, t // 4
                n = 8 * k + t
                if t % 4 == 0:
                    turn(pe, h, f"{name}.core")
                if n >= 1:
                    pe.wait_ge(x_e, n)
                for j in range(4):
                    m = min(512, SK - 512 * j)
                    last = nc.tensor.matmul(PQ[:, j, 0:m], W[:, t * P:(t + 1) * P], CT3[:, b, 512 * j:512 * j + m],
                                            start=True, stop=True)
                last.then_inc(x_s, 1)

            def weigh(t):
                b, h, n = t // 2, t // 4, 8 * k + t
                pe.wait_ge(x_e, n + 1)
                for g in range(4):
                    m = 4 * n + g
                    if m >= 2:
                        (pe.wait_ge(x_pta, (m - 2) // 2 + 1) if m % 2 == 0 else pe.wait_ge(x_ptd, (m - 2) // 2 + 1))
                    for j in range(4 * g, min(4 * g + 4, KT)):
                        rows = P if j < KT - 1 else KLAST
                        last = nc.tensor.transpose(PR[m % 2][0:rows, (j % 4) * P:(j % 4 + 1) * P],
                                                   PX3[:, t % 2, j * P:j * P + rows], ident)
                    last.then_inc(x_t, 1)
                pe.wait_ge(x_pta, 2 * n + 2)
                pe.wait_ge(x_ptd, 2 * n + 2)
                if t % 4:
                    pe.wait_ge(x_at, n)
                for j in range(KT):
                    rows = P if j < KT - 1 else KLAST
                    last = nc.tensor.matmul(PS[h][:, 0:P], PTX4[0:rows, t % 2, j, :], CN4[0:rows, b, j, :],
                                            start=(j == 0), stop=(j == KT - 1))
                last.then_inc(x_o, 1)
                pe.wait_ge(x_on, n + 1)
                nc.tensor.transpose(PS[h][:, P:2 * P], ONX3[:, t % 2, :], ident).then_inc(x_ot, 1)

            for t in range(8):
                scores(t)
                if t:
                    weigh(t - 1)
            weigh(7)

        def x_act(act, k):
            for t in range(9):
                if t < 8:
                    n = 8 * k + t
                    act.wait_ge(x_nb2, n + 1)
                    if n >= 2:
                        act.wait_ge(x_t, 4 * (n - 1))
                    nc.scalar.activation(PX3[:, t % 2, :], PQ[:, :, :].rearrange("p a b -> p (a b)")[:, 0:SK], ACT.Exp,
                                         bias=small[:, 16 + t:17 + t], scale=XSCALE,
                                         accum_out=small[:, 24 + t:25 + t]).then_inc(x_e, 1)
                if t:
                    n = 8 * k + t - 1
                    for g in (0, 2):
                        act.wait_ge(x_t, 4 * n + g + 1)
                        if n >= 2:
                            act.wait_ge(x_o, n - 1)
                        nc.scalar.activation(PTX4[:, (t - 1) % 2, 4 * g:4 * g + 4, :],
                                             PR[0][:, :].rearrange("p (j q) -> p j q", q=P), ACT.Copy).then_inc(x_pta, 1)
                    act.wait_ge(x_ot, n + 1)
                    nc.scalar.activation(XA[:, (t - 1) * P:t * P], PS[(t - 1) // 4][:, P:2 * P], ACT.Copy).then_inc(x_at, 1)

        def x_dve(dve, k):
            for t in range(9):
                if t < 8:
                    n = 8 * k + t
                    dve.wait_ge(x_s, n + 1)
                    nc.vector.tensor_reduce(small[:, t:t + 1], PQ[:, :, :].rearrange("p a b -> p (a b)")[:, 0:SK],
                                            AXX, ALU.max, negate=True).then_inc(x_mx, 1)
                    dve.wait_ge(x_mx, n + 1)
                    nc.vector.tensor_tensor(small[:, 8 + t:9 + t], small[:, t:t + 1], small[:, 40 + t:41 + t],
                                            ALU.subtract).then_inc(x_nb1, 1)
                    dve.wait_ge(x_nb1, n + 1)
                    nc.vector.tensor_scalar(small[:, 16 + t:17 + t], small[:, 8 + t:9 + t], small[:, 40 + t:41 + t],
                                            XSCALE, ALU.add, ALU.mult).then_inc(x_nb2, 1)
                if t:
                    n, u = 8 * k + t - 1, t - 1
                    for g in (1, 3):
                        dve.wait_ge(x_t, 4 * n + g + 1)
                        if n >= 2:
                            dve.wait_ge(x_o, n - 1)
                        if g == 1:
                            ins = nc.vector.tensor_copy(PTX4[:, u % 2, 4:8, :], PR[1][:, :].rearrange("p (j q) -> p j q", q=P))
                        else:
                            ins = nc.vector.tensor_copy(PTX4[0:KLAST, u % 2, 12, :], PR[1][0:KLAST, 0:P])
                        ins.then_inc(x_ptd, 1)
                    dve.wait_ge(x_e, n + 1)
                    nc.vector.reciprocal(small[:, 32 + u:33 + u], small[:, 24 + u:25 + u]).then_inc(x_rc, 1)
                    dve.wait_ge(x_rc, n + 1)
                    dve.wait_ge(x_o, n + 1)
                    if n >= 2:
                        dve.wait_ge(x_ot, n - 1)
                    nc.vector.tensor_scalar(ONX3[:, u % 2, :], PS[u // 4][:, 0:P], small[:, 32 + u:33 + u], None,
                                            ALU.mult).then_inc(x_on, 1)

        def PFS(n):
            return PF3[:, n, :].rearrange("p (q k) -> p q k", q=2)[:, :, 0:SEGF]

        F_BASE = len(CHAIN)
        F_END = F_BASE + DEPTH * len(LAYER)

        def fturn(eng, p, layer, name):
            eng.wait_ge(half[p], layer * len(LAYER) + (F_BASE + LAT[name]))

        SLOTS = 4 * CH // 2 + 8
        TAIL = ["wo", "woe", "shift2", "f.mean", "f.xc", "f.sq", "f.var", "f.rs", "f.out", "aff", "ffn0", "ffn1", "ffn2", "w2", "w2e"]

        def local_layers(eng, project, core, tail):
            project(0, 0, lambda slot: None)

            def tail_of(p, layer):
                return lambda slot: tail(TAIL[slot], p, layer) if slot < len(TAIL) else None

            with eng.Fori(0, DEPTH - 1) as layer:
                core(0, layer)
                project(1, layer, tail_of(0, layer))
                core(1, layer)
                project(0, layer + 1, tail_of(1, layer))
            core(0, DEPTH - 1)
            project(1, DEPTH - 1, tail_of(0, DEPTH - 1))
            core(1, DEPTH - 1)
            for name in TAIL:
                tail(name, 1, DEPTH - 1)

        @block.sync
        def _(sp):
            sp.dma_start(X[:, :], xT).then_inc(ld_x, 16)
            sp.dma_start(CST[:, :], cst).then_inc(ld_c, 16)
            sp.dma_start(W_A[:, :], wa).then_inc(ld_a, 16)
            sp.dma_start(VEC[:, :], vec).then_inc(ld_v, 16)
            sp.dma_start(REL[:, :], rel).then_inc(ld_rel, 16)
            sp.dma_start(CT, ctxT).then_inc(ld_ct, 16)
            sp.dma_start(W_B[:, :], wb).then_inc(ld_b, 16)
            for b in range(NB):
                sp.dma_start(CN4[:, b, 0:KT - 1, :], ctxN[b, 0:(KT - 1) * P, :].rearrange("(j p) d -> p j d", p=P)).then_inc(ld_cn, 16)
                sp.dma_start(CN4[0:KLAST, b, KT - 1, :], ctxN[b, (KT - 1) * P:SK, :]).then_inc(ld_cn, 16)
            sp.dma_start(MOE[:, 0:NE * FF], we1).then_inc(ld_moe, 16)
            sp.dma_start(MOE[:, NE * FF:2 * NE * FF], we2).then_inc(ld_moe, 16)
            sp.dma_start(CEN[:, :], cen).then_inc(ld_moe, 16)
            sp.dma_start(W_E[:, :], we).then_inc(ld_e, 16)
            sp.wait_ge(half[1], AT["B.mean"])
            sp.dma_start(REL[:, 0:3 * NH * DH + CH * P], wd).then_inc(ld_d, 16)
            sp.dma_start(LV6[:, :].rearrange("p (l n) -> p l n", l=DEPTH), lvec.rearrange("l p n -> p l n")).then_inc(ld_lv, 16)
            for h in HALVES:
                sp.wait_ge(half[h], AT["C.core"] + 1)
            sp.dma_start(WFQ, wfq[0, :, :]).then_inc(ld_fq, 16)
            sp.dma_start(LQ6, scl).then_inc(ld_fq, 16)
            sp.dma_start(WFO, wfo[0, :, :].rearrange("p (c d) -> p c d", c=CH)).then_inc(ld_fo, 16)
            sp.dma_start(WF1, wf1[0, :, :]).then_inc(ld_f1, 16)
            sp.dma_start(WF2, wf2[0, :, :].rearrange("p (j d) -> p j d", j=GT)).then_inc(ld_f1, 16)
            with sp.Fori(0, DEPTH - 1) as layer:
                fturn(sp, 1, layer, "core")
                sp.dma_start(WFQ, wfq[layer + 1, :, :]).then_inc(ld_fq, 16)
                fturn(sp, 1, layer, "woe")
                sp.dma_start(WFO, wfo[layer + 1, :, :].rearrange("p (c d) -> p c d", c=CH)).then_inc(ld_fo, 16)
                fturn(sp, 1, layer, "w2e")
                sp.dma_start(WF1, wf1[layer + 1, :, :]).then_inc(ld_f1, 16)
                sp.dma_start(WF2, wf2[layer + 1, :, :].rearrange("p (j d) -> p j d", j=GT)).then_inc(ld_f1, 16)
            for h in HALVES:
                sp.wait_ge(half[h], F_END + 1)
            sp.dma_start(out, X[:, :]).then_inc(stored, 16)
            sp.wait_ge(stored, 16)

        @block.gpsimd
        def _(pool):
            pool.wait_ge(ld_c, 16)
            for b in range(NB):
                for h in ((b // 2,) if b % 2 == 0 else ()):
                    pool.wait_ge(half[h], AT["A.ke"] + 1)
                if b >= 2:
                    pool.wait_ge(a_s, 16 * (b - 1))
                nc.gpsimd.tensor_tensor(KM4[:, b % 2, :, :],
                                        KA[:, b * SEQ:(b + 1) * SEQ].unsqueeze(1).to_broadcast([P, AH, SEQ]),
                                        head_mask.unsqueeze(2).to_broadcast([P, AH, SEQ]), ALU.mult).then_inc(a_km, 1)

            def f_project(p, layer, between):
                base = layer * 32 + 16 * p

                def add(v):
                    w, n, c = v // 8, v % 8 // 2, v % 2 * 512
                    dst = (KN3, QN3)[w][:, n, c:c + 512]
                    pool.wait_ge(f_t1, base + (v + 1))
                    nc.gpsimd.tensor_tensor(dst, dst, T2F3[:, v % 2, :], ALU.add).then_inc(f_add, 1)

                def normalise(n):
                    k = KN3[:, n, :].rearrange("p (h k) -> p h k", k=DH)
                    pool.wait_ge(f_rc1, layer * 4 + (2 * p + 1))
                    pool.wait_ge(f_add, base + 8)
                    nc.gpsimd.tensor_tensor(k, k, NRC[:, 0, n, :].unsqueeze(2).to_broadcast([P, NH, DH]), ALU.mult).then_inc(f_km, 1)

                for v in range(2 * 8):
                    add(v)
                    if v in (12, 15):
                        normalise(v // 15)
                normalise(2)
                normalise(3)

            local_layers(pool, f_project, lambda p, layer: None, lambda name, p, layer: None)

        @block.tensor
        def _(pe):
            pe.wait_ge(ld_x, 16)
            pe.wait_ge(ld_c, 16)
            ln_pe(pe, "A", X)
            pe.wait_ge(ld_a, 16)
            proj_pe(pe, "A.q", W_A[:, 0:P], XN)
            proj_pe(pe, "A.k", W_A[:, P:2 * P], XN)
            for h in HALVES:
                turn(pe, h, "A.v")
                for t in range(4):
                    last = nc.tensor.matmul(PS[h][:, t * P:(t + 1) * P], XN[:, h * HC + t * P:h * HC + (t + 1) * P],
                                            W_A[:, 2 * P:3 * P], start=True, stop=True)
                last.then_inc(half[h], 1)

            def a_scores(u):
                b, hp, q = u // 16, u // 2 % 8, u % 2
                if u % 16 == 0:
                    pe.wait_ge(half[b // 2], AT["A.ve"] + 1)
                    pe.wait_ge(a_km, b + 1)
                if u >= 2:
                    pe.wait_ge(a_ns, u - 1)
                nc.tensor.matmul(PQ[:, u % 2, :], QA[:, (2 * b + q) * P:(2 * b + q + 1) * P],
                                 KM4[:, b % 2, 2 * hp:2 * hp + 2, :], start=True, stop=True).then_inc(a_s, 1)

            def a_transpose(u):
                pe.wait_ge(a_e, u + 1)
                if u >= 2:
                    pe.wait_ge(a_pt, u - 1)
                for i in range(2):
                    for k in range(2):
                        last = nc.tensor.transpose(PR[u % 2][:, (2 * i + k) * P:(2 * i + k + 1) * P],
                                                   PA4[:, u % 2, i, k * P:(k + 1) * P], ident)
                last.then_inc(a_t, 1)

            def a_weigh(u):
                b, hp, q = u // 16, u // 2 % 8, u % 2
                pe.wait_ge(a_pt, u + 1)
                if u % 16 == 0 and b >= 2:
                    pe.wait_ge(half[(b - 2) // 2], AT[f"A.on{b % 2}"] + 1)
                for i in range(2):
                    c = q * P + (2 * hp + i) * ADK
                    for k in range(2):
                        last = nc.tensor.matmul(PQ[:, 2 + b % 2, c:c + ADK], PTA4[:, u % 2, 2 * i + k, :],
                                                VA3[:, 2 * b + k, (2 * hp + i) * ADK:(2 * hp + i + 1) * ADK],
                                                start=(k == 0), stop=(k == 1))
                last.then_inc(a_o, 1)

            def a_out(b):
                turn(pe, b // 2, f"A.ot{b % 2}")
                for q in range(2):
                    last = nc.tensor.transpose(PS[b // 2][:, q * P:(q + 1) * P], ON_A[:, b % 2, q, :], ident)
                last.then_inc(half[b // 2], 1)

            for u in range(64 + 2):
                if u < 64:
                    a_scores(u)
                if 0 <= u - 1 < 64:
                    a_transpose(u - 1)
                if u >= 2 and u - 2 < 64:
                    a_weigh(u - 2)
                if u >= 19 and (u - 19) % 16 == 0:
                    a_out((u - 19) // 16)
            a_out(3)

            ln_pe(pe, "B", X)
            pe.wait_ge(ld_b, 16)
            pe.wait_ge(ld_v, 16)
            proj_pe(pe, "B.h", W_B[:, 0:P], XN)
            proj_pe(pe, "B.q", W_B[:, P:2 * P], XI)
            proj_pe(pe, "B.u", W_B[:, 2 * P:3 * P], XQ)
            proj_pe(pe, "B.w", W_B[:, 3 * P:4 * P], XU)
            for h in HALVES:
                turn(pe, h, "B.s")
                for t in range(4):
                    c = h * HC + t * P
                    nc.tensor.matmul(PS[h][:, t:t + 1], XQ[:, c:c + P], VEC[:, V_KB:V_KB + 1], start=True, stop=False)
                    last = nc.tensor.matmul(PS[h][:, t:t + 1], XU[:, c:c + P], VEC[:, V_CB:V_CB + 1], start=False, stop=True)
                last.then_inc(half[h], 1)
            pe.wait_ge(ld_ct, 16)
            pe.wait_ge(ld_cn, 16 * 2 * NB)
            x_pe(pe, 0, XW)
            proj_pe(pe, "B.c", W_B[:, 4 * P:5 * P], XA)
            proj_pe(pe, "B.v", W_B[:, 5 * P:6 * P], XI)
            proj_pe(pe, "B.o", W_B[:, 6 * P:7 * P], XI)

            ln_pe(pe, "C", X)
            ln_pe(pe, "C2", XN)
            pe.wait_ge(ld_moe, 48)
            for h in HALVES:
                turn(pe, h, "C.lg")
                for t in range(4):
                    last = nc.tensor.matmul(PS[h][:, t * NE:(t + 1) * NE], XN[:, h * HC + t * P:h * HC + (t + 1) * P],
                                            CEN[:, :], start=True, stop=True)
                last.then_inc(half[h], 1)
            for e in range(NE):
                for h in HALVES:
                    turn(pe, h, f"C.bc{e}")
                    for t in range(4):
                        last = nc.tensor.matmul(PS[h][:, t * P:(t + 1) * P], OHT[:, h, t, e:e + 1].to_broadcast([P, P]),
                                                IDB[:, :], start=True, stop=True)
                    last.then_inc(half[h], 1)

            def w2(u):
                e = u // 2
                pe.wait_ge(c_r, 4 * u + 4)
                if u >= 2:
                    pe.wait_ge(c_ye, u - 1)
                for j in range(FT):
                    last = nc.tensor.matmul(PR[u % 2][:, :], W2M[:, e, j, :], HM4[:, u % 2, j, :], start=(j == 0), stop=(j == FT - 1))
                last.then_inc(c_y, 1)

            for u in range(2 * NE):
                e = u // 2
                pe.wait_ge(c_xe, u + 1)
                for j in range(FT):
                    if u:
                        pe.wait_ge(c_r, 4 * (u - 1) + j + 1)
                    nc.tensor.matmul(PQ[:, j, :], W1M[:, e, j * P:(j + 1) * P], XE3[:, u % 2, :], start=True, stop=True).then_inc(c_h, 1)
                if u:
                    w2(u - 1)
            w2(2 * NE - 1)

            ln_pe(pe, "D", X)
            ln_pe(pe, "D2", XN)
            pe.wait_ge(ld_d, 16)

            def d_project(g):
                if g == 0:
                    for h in HALVES:
                        turn(pe, h, "E.mean")
                for w in range(12):
                    n = 12 * g + w
                    bank = PQ[:, 2 + n % 2, :]
                    if w == 0 and g:
                        pe.wait_ge(d_res, 2 * g - 1)
                    if n >= 2:
                        pe.wait_ge(d_va if n % 2 == 0 else d_vd, n // 2)
                    if w < 8:
                        for k in range(2):
                            c = 2 * (w // 2) + k + (w % 2) * CH
                            last = nc.tensor.matmul(bank[:, k * 256:(k + 1) * 256], WDQ[:, c * P:(c + 1) * P],
                                                    XD[:, 256 * g:256 * (g + 1)], start=True, stop=True)
                    else:
                        b0 = 256 * g + P * ((w - 8) // 2)
                        last = nc.tensor.matmul(bank, XD[:, b0:b0 + P],
                                                WDQ[:, 2 * NH * DH + 512 * (w % 2):2 * NH * DH + 512 * (w % 2) + 512],
                                                start=True, stop=True)
                    last.then_inc(d_p, 1)

            for u in range(32 + 4):
                if u < 32:
                    g, n, q = u // 8, u // 4, u % 4
                    if u % 8 == 0:
                        d_project(g)
                        pe.wait_ge(d_va, 6 * (g + 1))
                        pe.wait_ge(d_vd, 6 * (g + 1))
                    if u >= 2:
                        pe.wait_ge(d_sub, u - 1)
                    nc.tensor.matmul(PQ[:, u % 2, :], IDB[:, :], MDB[:, :].unsqueeze(1).to_broadcast([P, 4, P]),
                                     start=True, stop=False)
                    for i in range(4):
                        r, c, b0 = 64 * (q % 2), 4 * (q // 2) + i, P * (n % 2)
                        last = nc.tensor.matmul(PQ[:, u % 2, i * P:(i + 1) * P], QD3[r:r + 64, c, b0:b0 + P],
                                                KD3[r:r + 64, c, b0:b0 + P], start=False, stop=(i == 3))
                    last.then_inc(d_s, 1)
                if 0 <= u - 1 < 32:
                    v = u - 1
                    job = d_job["p", v]
                    pe.wait_ge(d_e, v + 1)
                    if job >= 2:
                        pe.wait_ge(d_pt, job - 1)
                    for i in range(4):
                        last = nc.tensor.transpose(PR[job % 2][:, i * P:(i + 1) * P], PD4[:, v % 2, i, :], ident)
                    last.then_inc(d_t, 1)
                if 0 <= u - 2 < 32:
                    v = u - 2
                    pe.wait_ge(d_pt, d_job["p", v] + 1)
                    if v >= 2:
                        pe.wait_ge(d_on, v - 1)
                    for i in range(4):
                        last = nc.tensor.matmul(PS[v % 2][:, i * (DH + 1):(i + 1) * (DH + 1)], PTD4[:, v % 2, i, :],
                                                VD4[:, v // 4 % 4, 2 * (4 * (v % 4 // 2) + i) + v % 2, :], start=True, stop=True)
                    last.then_inc(d_o, 1)
                if u >= 6 and (u - 3) % 4 == 3:
                    n = (u - 3) // 4
                    pe.wait_ge(d_on, 4 * n + 4)
                    for g in range(2):
                        job = d_job["o", n, g]
                        pe.wait_ge(d_pt, job - 1)
                        for i in range(4):
                            c = 4 * g + i
                            last = nc.tensor.transpose(PR[job % 2][:, i * P:(i + 1) * P], OD3[:, n % 2, c * P:(c + 1) * P], ident)
                        last.then_inc(d_t, 1)
                    pe.wait_ge(d_pt, d_job["o", n, 1] + 1)
                    if n >= 2:
                        pe.wait_ge(d_res, n - 1)
                    for h in (d_va, d_vd):
                        pe.wait_ge(h, 6 * (min(u, 31) // 8 + 1))
                    for c in range(CH):
                        last = nc.tensor.matmul(PQ[:, 2 + n % 2, 0:P], WDO[:, c, :], OTD3[:, c, :], start=(c == 0), stop=(c == CH - 1))
                    last.then_inc(d_wo, 1)

            pe.wait_ge(d_res, 8)
            ln_pe(pe, "E", X)
            pe.wait_ge(ld_e, 16)
            proj_pe(pe, "E.q", W_E[:, 0:P], XN)
            proj_pe(pe, "E.w", W_E[:, P:2 * P], XQ)
            x_pe(pe, 1, XW)
            proj_pe(pe, "E.v", W_E[:, 2 * P:3 * P], XA)
            proj_pe(pe, "E.o", W_E[:, 3 * P:4 * P], XI)
            ln_pe(pe, "F", X)

            def f_project(p, layer, between):
                base = layer * 32 + 16 * p
                vb = layer * 8 + 4 * p
                fturn(pe, p, layer, "v")
                pe.wait_ge(ld_fq, layer * 16 + 32)
                for v in range(SLOTS):
                    w, n, c = v // 8, v % 8 // 2, v % 2 * 512
                    if 4 <= v < 20:
                        pe.wait_ge(f_t1, base + (v - 3))
                    if v >= 20:
                        pe.wait_ge(f_va if v % 2 == 0 else f_vd, vb + (v - 20) // 2 + 1)
                    w0 = (1, 0, 2)[w] * NH * DH + c
                    nc.tensor.matmul(PQ[:, v % 4, :], XSF[:, p * HC + n * P:p * HC + (n + 1) * P], WFQ[:, w0:w0 + 512],
                                     start=True, stop=True).then_inc(f_qp if v < 16 else f_v, 1)
                    between(v)

            def f_core(p, layer):
                base = layer * 64 + 32 * p
                jbase = layer * 96 + 48 * p
                kbase = layer * 32 + 16 * p
                pe.wait_ge(f_va, layer * 8 + (4 * p + 4))
                pe.wait_ge(f_vd, layer * 8 + (4 * p + 4))

                def transpose_qk(k):
                    j, c = k // 8, k % 8
                    pe.wait_ge(f_km, layer * 8 + (4 * p + 2 * j + 2))
                    if k == 0:
                        pe.wait_ge(f_add, layer * 32 + (16 * p + 16))
                        pe.wait_ge(half[p], layer * len(LAYER) + (F_BASE + LAT["core"]))
                    else:
                        pe.wait_ge(f_ke, kbase + k)
                    for i, src in enumerate((QN3, QN3, KN3, KN3)):
                        last = nc.tensor.transpose(PS[p][:, i * P:(i + 1) * P], src[:, 2 * j + i % 2, c * P:(c + 1) * P], ident)
                    last.then_inc(f_qt, 1)

                transpose_qk(0)
                for u in range(32 + 4):
                    if u < 32:
                        k = u // 2
                        if u % 2 == 0 and k + 1 < 16:
                            transpose_qk(k + 1)
                        pe.wait_ge(f_ke, kbase + (k + 1))
                        if u >= 2:
                            pe.wait_ge(f_sub, base + (u - 1))
                        nc.tensor.matmul(PQ[:, u % 2, 0:2 * SEGF], IDB[:, :], MFB[:, :], start=True, stop=False)
                        for q in range(2):
                            last = nc.tensor.matmul(PQ[:, u % 2, q * SEGF:(q + 1) * SEGF], QTF3[:, k % 2, q * P:(q + 1) * P],
                                                    KPF4[:, k % 2, u % 2, q * P:q * P + SEGF], start=False, stop=(q == 1))
                        last.then_inc(f_s, 1)
                    if 0 <= u - 2 < 32:
                        v = u - 2
                        job = f_job["p", v]
                        pe.wait_ge(f_e, base + (v + 1))
                        if job >= 2:
                            pe.wait_ge(f_pt, jbase + (job - 1))
                        for i in range(3):
                            last = nc.tensor.transpose(PR[job % 2][:, i * P:(i + 1) * P],
                                                       PF3[:, v % 3, WIN + i * P:WIN + (i + 1) * P], ident)
                        last.then_inc(f_t, 1)
                    if 0 <= u - 3 < 32:
                        v = u - 3
                        j, h, k = v // 16, v % 16, v // 2
                        pe.wait_ge(f_pt, jbase + (f_job["p", v] + 1))
                        if v % 2 == 0 and k >= 2:
                            pe.wait_ge(f_on, kbase + (k - 1))
                        o = PQ[:, 2 + k % 2, :]
                        for q, i, kt in ((0, 0, 0), (1, 1, 0), (1, 2, 1)):
                            c = (2 * q + h % 2) * (DH + 1)
                            last = nc.tensor.matmul(o[:, c:c + DH + 1], PTF4[:, v % 2, i, :], VF4[:, 2 * j + kt, h, :],
                                                    start=(i < 2), stop=(i != 1))
                        last.then_inc(f_o, 1)
                    if u >= 5 and u % 2 == 1:
                        k = (u - 4) // 2
                        job = f_job["o", k]
                        pe.wait_ge(f_on, kbase + (k + 1))
                        pe.wait_ge(f_pt, jbase + (job - 1))
                        for q in range(2):
                            last = nc.tensor.transpose(PR[job % 2][:, q * P:(q + 1) * P], ONF[:, k % 2, q, :], ident)
                        last.then_inc(f_t, 1)

            def f_tail(name, p, layer):
                xs = XSF[:, cols(p)]
                if name == "wo":
                    fturn(pe, p, layer, "wo")
                    pe.wait_ge(f_pt, layer * 96 + (48 * p + 48))
                    pe.wait_ge(ld_fo, layer * 16 + 16)
                    for c in range(CH):
                        last = nc.tensor.matmul(PS[p][:, :], WFO[:, c, :], OTF[:, c, :], start=(c == 0), stop=(c == CH - 1))
                    last.then_inc(half[p], 1)
                elif name in ("f.mean", "f.var"):
                    fturn(pe, p, layer, name)
                    src = xs if name == "f.mean" else SQ[:, cols(p)]
                    nc.tensor.matmul(PS[p][:, :], mean_w, src, start=True, stop=True).then_inc(half[p], 1)
                elif name.startswith("ffn"):
                    i = int(name[3])
                    m = min(P, GI - i * P)
                    if i == 0:
                        fturn(pe, p, layer, "ffn")
                        pe.wait_ge(ld_f1, layer * 32 + 32)
                    else:
                        pe.wait_ge(f_hh, layer * 6 + (3 * p + i))
                    nc.tensor.matmul(PR[0][0:m, :], WF1[:, GI + i * P:GI + i * P + m], xs, start=True, stop=True).then_inc(f_g, 1)
                    nc.tensor.matmul(PR[1][0:m, :], WF1[:, i * P:i * P + m], xs, start=True, stop=True).then_inc(f_a, 1)
                elif name == "w2":
                    fturn(pe, p, layer, "w2")
                    for i in range(GT):
                        m = min(P, GI - i * P)
                        last = nc.tensor.matmul(PS[p][:, :], WF2[0:m, i, :], HF3[0:m, i, :], start=(i == 0), stop=(i == GT - 1))
                    last.then_inc(half[p], 1)

            local_layers(pe, f_project, f_core, f_tail)

        @block.scalar
        def _(act):
            act.wait_ge(cast, 2)
            ln_act(act, "A", True)
            act.wait_ge(ld_v, 16)
            bias_act(act, "A.ke", KA, V_BK)
            bias_act(act, "A.ve", VA, None)
            for u in range(64):
                q = u % 2
                act.wait_ge(a_ns, u + 1)
                if u >= 2:
                    act.wait_ge(a_t, u - 1)
                for i in range(2):
                    h = 2 * (u // 2 % 8) + i
                    c = 64 + (u // 16 % 2) * 32 + q * AH + h
                    last = nc.scalar.activation(PA4[:, u % 2, i, :], NS4[:, u % 2, i, :], ACT.Exp, scale=-1.0,
                                                bias=small[:, 240 + 2 * (u % 4) + i:241 + 2 * (u % 4) + i],
                                                accum_out=small[:, c:c + 1])
                last.then_inc(a_e, 1)
            ln_act(act, "B", True)
            bias_act(act, "B.he", XI, V_HB)
            bias_act(act, "B.qe", XQ, V_QB)
            bias_act(act, "B.ue", XU, None)
            bias_act(act, "B.we", XW, None)
            x_act(act, 0)
            bias_act(act, "B.ce", XI, V_CB)
            ln_act(act, "C", True)
            ln_act(act, "C2", False)
            for e in range(NE):
                for h in HALVES:
                    turn(act, h, f"C.be{e}")
                    nc.scalar.activation(OH[:, e, cols(h)], PS[h][:, :], ACT.Copy).then_inc(half[h], 1)
            for u in range(2 * NE):
                for j in range(FT):
                    act.wait_ge(c_h, 4 * u + j + 1)
                    if u >= 2:
                        act.wait_ge(c_y, u - 1)
                    k = V_EB1 + (u // 2) * FT + j
                    nc.scalar.activation(HM4[:, u % 2, j, :], PQ[:, j, :], ACT.Relu, bias=VEC[:, k:k + 1]).then_inc(c_r, 1)

            ln_act(act, "D", False)
            ln_act(act, "D2", False)

            def d_evac(g):
                for w in range(0, 12, 2):
                    act.wait_ge(d_p, 12 * g + w + 1)
                    if w < 8:
                        dst = QD3[:, w:w + 2, :].rearrange("p c t -> p (c t)")
                        src = PQ[:, 2, :]
                    else:
                        dst = VD4[:, (2 * g + (w - 8) // 2) % 4, 0:8, 0:DH]
                        src = PQ[:, 2, :].rearrange("p (h k) -> p h k", k=DH)
                    nc.scalar.activation(dst, src, ACT.Copy).then_inc(d_va, 1)

            act.wait_ge(d_one, 1)
            for u in range(32 + 4):
                if u < 32:
                    if u % 8 == 0:
                        d_evac(u // 8)
                    act.wait_ge(d_sub, u + 1)
                    nc.scalar.activation(PD4[:, u % 2, :, :], PD4[:, u % 2, :, :], ACT.Exp, scale=XSCALE).then_inc(d_e, 1)
                if 0 <= u - 1 < 32:
                    v = u - 1
                    job = d_job["p", v]
                    act.wait_ge(d_t, job + 1)
                    if v >= 2:
                        act.wait_ge(d_o, v - 1)
                    nc.scalar.activation(PTD4[:, v % 2, :, :], PR[job % 2][:, :].rearrange("p (i q) -> p i q", i=4),
                                         ACT.Copy).then_inc(d_pt, 1)
                if u >= 6 and (u - 3) % 4 == 3:
                    n = (u - 3) // 4
                    for g in range(2):
                        job = d_job["o", n, g]
                        act.wait_ge(d_t, job + 1)
                        if n:
                            act.wait_ge(d_wo, n)
                        nc.scalar.activation(OTD3[:, 4 * g:4 * g + 4, :], PR[job % 2][:, :].rearrange("p (i q) -> p i q", i=4),
                                             ACT.Copy).then_inc(d_pt, 1)

            ln_act(act, "E", False)
            bias_act(act, "E.qe", XQ, None)
            bias_act(act, "E.we", XW, None)
            x_act(act, 1)
            bias_act(act, "E.ve", XI, None)
            ln_act(act, "F", False)

            def f_project(p, layer, between):
                base = layer * 32 + 16 * p
                for v in range(SLOTS):
                    if v < 16:
                        act.wait_ge(f_qp, base + (v + 1))
                        if v >= 2:
                            act.wait_ge(f_red, base + (v - 1))
                        nc.scalar.activation(SQF3[:, v % 2, :], PQ[:, v % 4, :], ACT.Square).then_inc(f_sq, 1)
                    elif v % 2 == 0:
                        act.wait_ge(f_v, layer * 16 + (8 * p + v - 15))
                        nc.scalar.activation(VF4[:, (v - 16) // 2, 0:8, 0:DH], PQ[:, v % 4, :].rearrange("p (h k) -> p h k", k=DH),
                                             ACT.Copy).then_inc(f_va, 1)
                    if v in (8, 16):
                        w = v // 16
                        act.wait_ge(f_red, base + v)
                        nc.scalar.activation(NRM[:, w, :, :], NSQ[:, w, :, :], ACT.Sqrt).then_inc(f_nrm, 1)
                    between(v)

            def f_core(p, layer):
                base = layer * 64 + 32 * p
                jbase = layer * 96 + 48 * p
                kbase = layer * 32 + 16 * p

                def take_qk(k):
                    act.wait_ge(f_qt, kbase + (k + 1))
                    if k >= 2:
                        act.wait_ge(f_s, base + (2 * k - 2))
                    nc.scalar.activation(QTF3[:, k % 2, :], PS[p][:, 0:SEQ], ACT.Copy)
                    for r in range(2):
                        rows = slice(64 * r, 64 * r + 64)
                        last = nc.scalar.activation(KPF4[rows, k % 2, r, WIN:WIN + SEQ], PS[p][rows, SEQ:2 * SEQ], ACT.Copy)
                    last.then_inc(f_ke, 1)

                take_qk(0)
                for u in range(32 + 4):
                    if u < 32:
                        if u % 2 == 0 and u // 2 + 1 < 16:
                            take_qk(u // 2 + 1)
                        act.wait_ge(f_sub, base + (u + 1))
                        nc.scalar.activation(PFS(u % 3), PFS(u % 3), ACT.Exp, scale=QK_SCALE).then_inc(f_e, 1)
                    if 0 <= u - 2 < 32:
                        v = u - 2
                        job = f_job["p", v]
                        act.wait_ge(f_t, jbase + (job + 1))
                        if v >= 2:
                            act.wait_ge(f_o, base + (v - 1))
                        nc.scalar.activation(PTF4[:, v % 2, :, :], PR[job % 2][:, 0:3 * P].rearrange("p (i q) -> p i q", i=3),
                                             ACT.Copy).then_inc(f_pt, 1)
                    if u >= 5 and u % 2 == 1:
                        k = (u - 4) // 2
                        job = f_job["o", k]
                        act.wait_ge(f_t, jbase + (job + 1))
                        nc.scalar.activation(OTF[:, k % 8, (k // 8) * SEQ:(k // 8 + 1) * SEQ], PR[job % 2][:, 0:SEQ],
                                             ACT.Copy).then_inc(f_pt, 1)

            def f_tail(name, p, layer):
                if name == "f.sq":
                    fturn(act, p, layer, name)
                    nc.scalar.activation(SQ[:, cols(p)], XC[:, cols(p)], ACT.Square).then_inc(half[p], 1)
                elif name == "f.rs":
                    fturn(act, p, layer, name)
                    nc.scalar.activation(RS[:, cols(p)], PS[p][:, :], ACT.Abs_reciprocal_sqrt, bias=eps_ap).then_inc(half[p], 1)
                elif name.startswith("ffn"):
                    i = int(name[3])
                    m = min(P, GI - i * P)
                    act.wait_ge(f_g, layer * 6 + (3 * p + i + 1))
                    nc.scalar.activation(GF3[0:m, i, :], PR[0][0:m, :], ACT.Gelu, bias=LV[0:m, L_B1G + i:L_B1G + i + 1]).then_inc(f_ge, 1)

            local_layers(act, f_project, f_core, f_tail)

        @block.vector
        def _(dve):
            dve.wait_ge(ld_c, 16)
            nc.vector.tensor_copy(IDB[:, :], ident).then_inc(cast, 1)
            nc.vector.memset(small[:, 224:256], EPS).then_inc(cast, 1)
            nc.vector.memset(small[:, 0:192], 0.0).then_inc(cast, 1)
            nc.vector.tensor_copy(MDB[:, :], CST[:, C_MD:C_MD + P]).then_inc(cast, 1)
            nc.vector.tensor_copy(MFB[:, :], CST[:, C_MF:C_MF + 2 * SEGF]).then_inc(cast, 1)
            dve.wait_ge(cast, 3)
            ln_dve(dve, "A", X, XN, True)
            dve.wait_ge(ld_v, 16)
            for h in HALVES:
                turn(dve, h, "A.qe")
                nc.vector.tensor_scalar(QA[:, cols(h)], PS[h][:, :], VEC[:, V_BQ:V_BQ + 1], ADK ** -0.5,
                                        ALU.add, ALU.mult).then_inc(half[h], 1)
            dve.wait_ge(ld_rel, 16)

            def a_out(b):
                h, j = b // 2, b % 2
                r = small[:, 128 + 32 * j:160 + 32 * j]
                turn(dve, h, f"A.rc{j}")
                dve.wait_ge(a_e, 16 * (b + 1))
                nc.vector.reciprocal(r, small[:, 64 + 32 * j:96 + 32 * j]).then_inc(half[h], 1)
                turn(dve, h, f"A.on{j}")
                dve.wait_ge(a_o, 16 * (b + 1))
                nc.vector.tensor_tensor(ON_A[:, j, :, :].rearrange("p q (h k) -> p (q h) k", k=ADK),
                                        PQ[:, 2 + j, 0:2 * P].rearrange("p (x k) -> p x k", k=ADK),
                                        r.unsqueeze(2).to_broadcast([P, 2 * AH, ADK]), ALU.mult).then_inc(half[h], 1)

            def a_residual(b):
                h, j = b // 2, b % 2
                turn(dve, h, f"A.res{j}")
                x = X[:, b * SEQ:(b + 1) * SEQ]
                nc.vector.scalar_tensor_tensor(x, PS[h][:, 0:SEQ], VEC[:, V_BV:V_BV + 1], x, ALU.add, ALU.add).then_inc(half[h], 1)

            for u in range(64 + 2):
                if u < 64:
                    q = u % 2
                    dve.wait_ge(a_s, u + 1)
                    if u >= 2:
                        dve.wait_ge(a_e, u - 1)
                    for i in range(2):
                        h = 2 * (u // 2 % 8) + i
                        last = nc.vector.tensor_tensor_reduce(
                            out=NS4[:, u % 2, i, :], in0=PQ[:, u % 2, i * SEQ:(i + 1) * SEQ],
                            in1=rel3[:, h, P - q * P:P - q * P + SEQ], scale=-1.0, scalar=BIG,
                            op0=ALU.add, op1=ALU.min, accum_out=small[:, 240 + 2 * (u % 4) + i:241 + 2 * (u % 4) + i])
                    last.then_inc(a_ns, 1)
                if u >= 1 and u - 1 < 64:
                    v = u - 1
                    dve.wait_ge(a_t, v + 1)
                    if v >= 2:
                        dve.wait_ge(a_o, v - 1)
                    nc.vector.tensor_copy(PTA4[:, v % 2, :, :], PR[v % 2][:, :].rearrange("p (j q) -> p j q", j=4)).then_inc(a_pt, 1)
                if u >= 18 and (u - 18) % 16 == 0:
                    a_out((u - 18) // 16)
                if u >= 20 and (u - 20) % 16 == 0:
                    a_residual((u - 20) // 16)
            a_out(3)
            a_residual(3)

            ln_dve(dve, "B", X, XN, True)
            for h in HALVES:
                turn(dve, h, "B.se")
                nc.vector.tensor_copy(small[:, 40 + 4 * h:44 + 4 * h], PS[h][:, 0:4]).then_inc(half[h], 1)
            x_dve(dve, 0)
            for h in HALVES:
                turn(dve, h, "B.core")
                dve.wait_ge(x_at, 4 * (h + 1))
                nc.vector.memset(small[:, 48 + h:49 + h], 0.0).then_inc(half[h], 1)
            add_dve(dve, "B.ve", XI, V_VB, XQ)
            add_dve(dve, "B.oe", X, V_OB, X)

            ln_dve(dve, "C", X, XN, True)
            ln_dve(dve, "C2", XN, XI, False)
            for h in HALVES:
                turn(dve, h, "C.addx")
                nc.vector.tensor_tensor(X[:, cols(h)], X[:, cols(h)], XN[:, cols(h)], ALU.add).then_inc(half[h], 1)
            for h in HALVES:
                lg = small[:, 64 + 32 * h:96 + 32 * h].rearrange("p (a e) -> p a e", e=NE)
                mx = small[:, 128 + 8 * h:132 + 8 * h]
                m2 = small[:, 132 + 8 * h:136 + 8 * h]
                ps = PS[h][:, 0:32].rearrange("p (a e) -> p a e", e=NE)
                turn(dve, h, "C.mx")
                nc.vector.tensor_reduce(mx, ps, AXX, ALU.max).then_inc(half[h], 1)
                turn(dve, h, "C.eq")
                nc.vector.tensor_tensor(lg, ps, mx.unsqueeze(2).to_broadcast([P, 4, NE]), ALU.is_equal).then_inc(half[h], 1)
                turn(dve, h, "C.pr")
                nc.vector.tensor_tensor(lg, lg, prio, ALU.mult).then_inc(half[h], 1)
                turn(dve, h, "C.m2")
                nc.vector.tensor_reduce(m2, lg, AXX, ALU.max).then_inc(half[h], 1)
                turn(dve, h, "C.oh")
                nc.vector.tensor_tensor(OHT[:, h, :, :], lg, m2.unsqueeze(2).to_broadcast([P, 4, NE]), ALU.is_equal).then_inc(half[h], 1)

            def expert_in(u):
                e, h = u // 2, u % 2
                if u < 2:
                    dve.wait_ge(half[h], AT["C.core"])
                else:
                    dve.wait_ge(c_h, 4 * (u - 1))
                nc.vector.tensor_scalar(XE3[:, u % 2, :], XI[:, cols(h)], VEC[:, V_EG + e:V_EG + e + 1],
                                        VEC[:, V_EB + e:V_EB + e + 1], ALU.mult, ALU.add).then_inc(c_xe, 1)

            expert_in(0)
            for u in range(2 * NE):
                e, h = u // 2, u % 2
                if u + 1 < 2 * NE:
                    expert_in(u + 1)
                dve.wait_ge(c_y, u + 1)
                if u >= 2:
                    dve.wait_ge(c_acc, u - 1)
                nc.vector.scalar_tensor_tensor(YE3[:, u % 2, :], PR[u % 2][:, :], VEC[:, V_EB2 + e:V_EB2 + e + 1],
                                               OH[:, e, cols(h)], ALU.add, ALU.mult).then_inc(c_ye, 1)
                dve.wait_ge(c_ye, u + 1)
                nc.vector.tensor_tensor(X[:, cols(h)], X[:, cols(h)], YE3[:, u % 2, :], ALU.add).then_inc(c_acc, 1)
            for h in HALVES:
                dve.wait_ge(c_acc, 2 * NE)
                turn(dve, h, "C.core")
                nc.vector.memset(small[:, 48 + h:49 + h], 0.0).then_inc(half[h], 1)

            ln_dve(dve, "D", X, XN, False)
            ln_dve(dve, "D2", XN, XI, False)
            for h in HALVES:
                turn(dve, h, "D.addx")
                nc.vector.tensor_tensor(X[:, cols(h)], X[:, cols(h)], XN[:, cols(h)], ALU.add).then_inc(half[h], 1)
            for h in HALVES:
                turn(dve, h, "D.aff")
                nc.vector.tensor_scalar(XD4[:, :, 2 * h:2 * h + 2, :], XI[:, cols(h)].rearrange("p (i n b) -> p n i b", i=2, n=8),
                                        VEC[:, V_LW:V_LW + 1], VEC[:, V_LB:V_LB + 1], ALU.mult, ALU.add).then_inc(half[h], 1)
            nc.vector.memset(VD4[:, :, :, DH:DH + 1], 1.0).then_inc(d_one, 1)

            def d_evac(g):
                for w in range(1, 12, 2):
                    dve.wait_ge(d_p, 12 * g + w + 1)
                    if w < 8:
                        ins = nc.vector.tensor_copy(KD3[:, w - 1:w + 1, :].rearrange("p c t -> p (c t)"), PQ[:, 3, :])
                    else:
                        ins = nc.vector.tensor_copy(VD4[:, (2 * g + (w - 8) // 2) % 4, 8:16, 0:DH],
                                                    PQ[:, 3, :].rearrange("p (h k) -> p h k", k=DH))
                    ins.then_inc(d_vd, 1)

            X4 = X[:, :].rearrange("p (i b) -> p i b", i=4)
            for u in range(32 + 5):
                if u < 32:
                    if u % 8 == 0:
                        d_evac(u // 8)
                    mx = small[:, 64 + 4 * (u % 2):68 + 4 * (u % 2)]
                    s4 = PQ[:, u % 2, :].rearrange("p (i k) -> p i k", i=4)
                    dve.wait_ge(d_s, u + 1)
                    nc.vector.tensor_reduce(mx, s4, AXX, ALU.max).then_inc(d_mx, 1)
                    dve.wait_ge(d_mx, u + 1)
                    if u >= 2:
                        dve.wait_ge(d_t, d_job["p", u - 2] + 1)
                    nc.vector.tensor_tensor(PD4[:, u % 2, :, :], s4, mx.unsqueeze(2).to_broadcast([P, 4, P]),
                                            ALU.subtract).then_inc(d_sub, 1)
                if 0 <= u - 2 < 32:
                    v = u - 2
                    n = v // 4
                    rc = small[:, 72 + 4 * (v % 2):76 + 4 * (v % 2)]
                    o4 = PS[v % 2][:, 0:4 * (DH + 1)].rearrange("p (i k) -> p i k", i=4)
                    dve.wait_ge(d_o, v + 1)
                    nc.vector.reciprocal(rc.unsqueeze(2), o4[:, :, DH:DH + 1]).then_inc(d_rc, 1)
                    dve.wait_ge(d_rc, v + 1)
                    if n >= 2:
                        dve.wait_ge(d_t, d_job["o", n - 2, 1] + 1)
                    nc.vector.tensor_tensor(OD3[:, n % 2, :].rearrange("p (c r k) -> p r c k", r=2, k=DH)[:, v % 2, 4 * (v % 4 // 2):4 * (v % 4 // 2) + 4, :],
                                            o4[:, :, 0:DH], rc.unsqueeze(2).to_broadcast([P, 4, DH]), ALU.mult).then_inc(d_on, 1)
                if u >= 6 and (u - 3) % 4 == 3 and u - 3 < 32:
                    n = (u - 3) // 4
                    x4 = X4[:, :, 32 * n:32 * n + 32]
                    dve.wait_ge(d_wo, n + 1)
                    nc.vector.tensor_tensor(x4, x4, PQ[:, 2 + n % 2, 0:P].rearrange("p (i b) -> p i b", i=4), ALU.add).then_inc(d_res, 1)

            dve.wait_ge(d_res, 8)
            ln_dve(dve, "E", X, XN, False)
            nc.vector.memset(small[:, 40:48], 0.0).then_inc(cast, 1)
            dve.wait_ge(cast, 6)
            x_dve(dve, 1)
            for h in HALVES:
                turn(dve, h, "E.core")
                dve.wait_ge(x_at, 8 + 4 * (h + 1))
                nc.vector.memset(small[:, 48 + h:49 + h], 0.0).then_inc(half[h], 1)
            add_dve(dve, "E.oe", X, None, X)
            ln_dve(dve, "F", X, YF, False)
            nc.vector.memset(KPF, 0.0).then_inc(f_lv, 1)
            nc.vector.memset(VF4[:, :, :, DH:DH + 1], 1.0).then_inc(f_lv, 1)
            nc.vector.memset(PF3[:, :, SEGF:256], 0.0).then_inc(f_lv, 1)
            dve.wait_ge(f_lv, 3)
            dve.wait_ge(ld_lv, 16)
            dve.wait_ge(ld_fq, 32)

            def shift(p):
                y, xs = (z[:, cols(p)].rearrange("p (j t) -> p j t", j=2) for z in (YF, XSF))
                nc.vector.tensor_copy(xs[0:64], y[0:64])
                nc.vector.memset(xs[64:128, :, 0:1], 0.0)
                return nc.vector.tensor_copy(xs[64:128, :, 1:SEQ], y[64:128, :, 0:SEQ - 1])

            def f_project(p, layer, between):
                base = layer * 32 + 16 * p
                fturn(dve, p, layer, "shift")
                shift(p).then_inc(half[p], 1)
                if p == 0:
                    nc.vector.tensor_tensor(TABF, CST[:, C_ROT:C_ROT + 4 * P].rearrange("p (n q d) -> p n q d", n=4, q=2),
                                            LQ6[:, bass.ds(layer * (4 * DH), 4 * DH)].rearrange("p (n d) -> p n d", n=4)
                                            .unsqueeze(2).to_broadcast([P, 4, 2, DH]), ALU.mult).then_inc(f_tab, 1)
                    dve.wait_ge(f_tab, layer + 1)
                for v in range(SLOTS):
                    if v < 16:
                        w, n, c = v // 8, v % 8 // 2, v % 2
                        raw = PQ[:, v % 4, :].rearrange("p (h s k) -> p h s k", s=2, k=DH // 2)
                        tab = [TABF[:, 2 * (1 - w) + z, n % 2, :].rearrange("p (s k) -> p s k", s=2) for z in range(2)]
                        t1 = (KN3, QN3)[w][:, n, c * 512:(c + 1) * 512].rearrange("p (h s k) -> p h s k", s=2, k=DH // 2)
                        t2 = T2F3[:, v % 2, :].rearrange("p (h s k) -> p h s k", s=2, k=DH // 2)
                        dve.wait_ge(f_sq, base + (v + 1))
                        nc.vector.tensor_reduce(NSQ[:, w, n, 8 * c:8 * c + 8], SQF3[:, v % 2, :].rearrange("p (h k) -> p h k", k=DH),
                                                AXX, ALU.add).then_inc(f_red, 1)
                        if v >= 2:
                            dve.wait_ge(f_add, base + (v - 1))
                        for s in range(2):
                            last = nc.vector.tensor_tensor(t2[:, :, s, :], raw[:, :, 1 - s, :],
                                                           tab[1][:, s, :].unsqueeze(1).to_broadcast([P, 8, DH // 2]), ALU.mult)
                        last.then_inc(f_t2, 1)
                        nc.vector.tensor_tensor(t1.rearrange("p h s k -> p h (s k)"), raw.rearrange("p h s k -> p h (s k)"),
                                                TABF[:, 2 * (1 - w), n % 2, :].unsqueeze(1).to_broadcast([P, 8, DH]),
                                                ALU.mult).then_inc(f_t1, 1)
                    elif v % 2:
                        dve.wait_ge(f_v, layer * 16 + (8 * p + v - 15))
                        nc.vector.tensor_copy(VF4[:, (v - 16) // 2, 8:16, 0:DH], PQ[:, v % 4, :].rearrange("p (h k) -> p h k", k=DH)).then_inc(f_vd, 1)
                    if v in (9, 17):
                        w = v // 17
                        m = layer * 4 + (2 * p + w + 1)
                        dve.wait_ge(f_nrm, m)
                        nc.vector.tensor_scalar(NRM[:, w, :, :], NRM[:, w, :, :], 1e-12, None, ALU.max).then_inc(f_gd, 1)
                        dve.wait_ge(f_gd, m)
                        nc.vector.reciprocal(NRC[:, w, :, :], NRM[:, w, :, :]).then_inc(f_rc1, 1)
                    between(v)
                fturn(dve, p, layer, "v")
                dve.wait_ge(f_vd, layer * 8 + (4 * p + 4))
                dve.wait_ge(f_rc1, layer * 4 + (2 * p + 2))
                nc.vector.memset(small[:, 48:49], 0.0).then_inc(half[p], 1)

            def f_core(p, layer):
                base = layer * 64 + 32 * p
                jbase = layer * 96 + 48 * p
                kbase = layer * 32 + 16 * p
                for u in range(32 + 4):
                    if u < 32:
                        mx = small[:, 64 + 2 * (u % 2):66 + 2 * (u % 2)]
                        s2 = PQ[:, u % 2, 0:2 * SEGF].rearrange("p (q k) -> p q k", q=2)
                        dve.wait_ge(f_s, base + (u + 1))
                        nc.vector.tensor_reduce(mx, s2, AXX, ALU.max).then_inc(f_mx, 1)
                        dve.wait_ge(f_mx, base + (u + 1))
                        if u >= 3:
                            dve.wait_ge(f_t, jbase + (f_job["p", u - 3] + 1))
                        for q in range(2):
                            last = nc.vector.tensor_scalar(PFS(u % 3)[:, q, :], s2[:, q, :], mx[:, q:q + 1],
                                                           NRC[:, 1, 2 * (u // 16) + q, u % 16:u % 16 + 1], ALU.subtract, ALU.mult)
                        last.then_inc(f_sub, 1)
                    if u >= 4 and u % 2 == 0 and u - 3 < 32:
                        k = (u - 3) // 2
                        rc = small[:, 72 + 4 * (k % 2):76 + 4 * (k % 2)]
                        o4 = PQ[:, 2 + k % 2, 0:4 * (DH + 1)].rearrange("p (i k) -> p i k", i=4)
                        dve.wait_ge(f_o, base + (2 * k + 2))
                        nc.vector.reciprocal(rc.unsqueeze(2), o4[:, :, DH:DH + 1]).then_inc(f_rc, 1)
                        dve.wait_ge(f_rc, kbase + (k + 1))
                        if k >= 2:
                            dve.wait_ge(f_t, jbase + (f_job["o", k - 2] + 1))
                        nc.vector.tensor_tensor(ONF[:, k % 2, :, :].rearrange("p q (i k) -> p (q i) k", k=DH), o4[:, :, 0:DH],
                                                rc.unsqueeze(2).to_broadcast([P, 4, DH]), ALU.mult).then_inc(f_on, 1)
                fturn(dve, p, layer, "core")
                nc.vector.memset(small[:, 48:49], 0.0).then_inc(half[p], 1)

            def f_tail(name, p, layer):
                xs, y, xc = XSF[:, cols(p)], YF[:, cols(p)], XC[:, cols(p)]
                if name in ("woe", "shift2", "f.xc", "f.out", "aff", "w2e"):
                    fturn(dve, p, layer, name)
                if name == "woe":
                    nc.vector.tensor_tensor(y, y, PS[p][:, :], ALU.add).then_inc(half[p], 1)
                    if p == 0:
                        nc.vector.tensor_copy(LV[:, :], LV6[:, bass.ds(layer * NLV, NLV)]).then_inc(f_lv, 1)
                elif name == "shift2":
                    shift(p).then_inc(half[p], 1)
                elif name == "f.xc":
                    nc.vector.tensor_tensor(xc, xs, PS[p][:, :], ALU.subtract).then_inc(half[p], 1)
                elif name == "f.out":
                    nc.vector.tensor_tensor(xs, xc, RS[:, cols(p)], ALU.mult).then_inc(half[p], 1)
                elif name == "aff":
                    dve.wait_ge(f_lv, layer + 4)
                    nc.vector.tensor_scalar(xs, xs, LV[:, L_G:L_G + 1], LV[:, L_B:L_B + 1], ALU.mult, ALU.add).then_inc(half[p], 1)
                elif name.startswith("ffn"):
                    i = int(name[3])
                    m = min(P, GI - i * P)
                    dve.wait_ge(f_ge, layer * 6 + (3 * p + i + 1))
                    dve.wait_ge(f_a, layer * 6 + (3 * p + i + 1))
                    nc.vector.scalar_tensor_tensor(HF3[0:m, i, :], PR[1][0:m, :], LV[0:m, L_B1A + i:L_B1A + i + 1], GF3[0:m, i, :],
                                                   ALU.add, ALU.mult).then_inc(f_hh, 1)
                    if i == GT - 1:
                        fturn(dve, p, layer, "ffn")
                        dve.wait_ge(f_hh, layer * 6 + (3 * p + 3))
                        nc.vector.memset(small[:, 48:49], 0.0).then_inc(half[p], 1)
                elif name == "w2e":
                    nc.vector.scalar_tensor_tensor(y, PS[p][:, :], LV[:, L_B2:L_B2 + 1], y, ALU.add, ALU.add).then_inc(half[p], 1)

            local_layers(dve, f_project, f_core, f_tail)
            for h in HALVES:
                dve.wait_ge(half[h], F_END)
                nc.vector.tensor_tensor(X[:, cols(h)], X[:, cols(h)], YF[:, cols(h)], ALU.add).then_inc(half[h], 1)


def kernel(**inputs):
    import numpy as np
    import concourse.bacc as _bacc
    from concourse import mybir as _mybir
    from concourse.bass_utils import run_bass_kernel_spmd as _run

    i = {k: np.asarray(v) for k, v in inputs.items()}
    f = np.float32

    def cols(*vs):
        return np.stack(vs, axis=1)

    cst = np.zeros((P, NCST), f)
    cst[:, C_ID:C_ID + P] = np.eye(P)
    cst[:, C_MEAN:C_MEAN + P] = 1.0 / P
    p = np.arange(P)
    cst[:, C_BLK:C_BLK + P] = (p[:, None] // DH == p[None, :] // DH)
    cst[:, C_HM:C_HM + AH] = (p[:, None] // ADK == np.arange(AH)[None, :])
    cst[:, C_PR:C_PR + 4 * NE] = np.tile(NE - np.arange(NE), 4)[None, :]
    cst[:, C_MD:C_MD + P] = np.where(p[:, None] % 32 == p[None, :] % 32, 0.0, -1e30)
    for q in range(2):
        it = q * P + p[:, None]
        jt = q * P - WIN + np.arange(SEGF)[None, :]
        ok = (jt >= 0) & (it >= jt) & (it <= jt + WIN)
        cst[:, C_MF + q * SEGF:C_MF + (q + 1) * SEGF] = np.where(ok, 0.0, -1e30)
    hd = np.arange(0, DH, 2, dtype=f)
    inv = (1.0 / f(10000.0) ** (hd / f(DH))).astype(f)
    t = np.arange(SEQ, dtype=f)
    fr = (t[:, None] * inv[None, :]).astype(f)
    base = ((hd + f(0.4 * DH)) / f(1.4 * DH)).astype(f)
    sc = (base[None, :] ** ((t - SEQ // 2) / f(WIN // 2))[:, None]).astype(f)
    fr, sc = (np.concatenate([z, z], 1) for z in (fr, sc))
    sign = np.where(np.arange(DH) < DH // 2, -1.0, 1.0).astype(f)
    rot = [np.cos(fr) * sc, np.sin(fr) * sc * sign, np.cos(fr) / sc, np.sin(fr) / sc * sign]
    for n, r in enumerate(rot):
        cst[:, C_ROT + n * P:C_ROT + (n + 1) * P] = r.reshape(2, P, DH).transpose(1, 0, 2).reshape(P, P)

    vec = np.zeros((P, NVEC), f)
    for c, n in ((V_BQ, 'L0_attn_bq'), (V_BK, 'L0_attn_bk'), (V_BV, 'L0_attn_bv'), (V_HB, 'L0_xattn_hb'), (V_QB, 'L0_xattn_qb'),
                 (V_KB, 'L0_xattn_kb'), (V_CB, 'L0_xattn_cb'), (V_VB, 'L0_xattn_vb'), (V_OB, 'L0_xattn_ob'),
                 (V_LW, 'L1_attn_ln_w'), (V_LB, 'L1_attn_ln_b')):
        vec[:, c] = i[n]
    vec[:, V_EG:V_EG + NE] = i['L0_ffn_ln_g'].T
    vec[:, V_EB:V_EB + NE] = i['L0_ffn_ln_b'].T
    vec[:, V_EB2:V_EB2 + NE] = i['L0_ffn_b2'].T
    vec[:, V_EB1:] = i['L0_ffn_b1'].reshape(NE * FT, P).T
    rel = i['L0_attn_rel_emb'][:, ::-1]
    band = P - 1 - p[:, None] + np.arange(3 * P)[None, :]
    band = np.minimum(band, 2 * SEQ - 2)
    x = i['L0_xattn_hW'], i['L0_xattn_qW'], i['L0_xattn_kW'], i['L0_xattn_cW'], i['L0_xattn_vW'], i['L0_xattn_oW']
    wd = i['L1_attn_w_qkv'].reshape(NH, 3, DH, P).transpose(3, 1, 0, 2).reshape(P, 3 * NH * DH)
    wdo = i['L1_attn_w_out'].T.reshape(CH, P, P).transpose(1, 0, 2).reshape(P, CH * P)
    wq = i['L1_ffn_Wqkv']
    lvec = np.zeros((DEPTH, P, NLV), f)
    lvec[:, :, L_G], lvec[:, :, L_B], lvec[:, :, L_B2] = i['L1_ffn_ln_g'], i['L1_ffn_ln_b'], i['L1_ffn_b2']
    b1 = np.zeros((DEPTH, 2, GT * P), f)
    b1[:, :, :GI] = i['L1_ffn_b1'].reshape(DEPTH, 2, GI)
    lvec[:, :, L_B1A:L_B1A + 2 * GT] = b1.reshape(DEPTH, 2 * GT, P).transpose(0, 2, 1)
    qs, ks = i['L1_ffn_q_scale'], i['L1_ffn_k_scale']
    half_swap = (np.arange(DH) + DH // 2) % DH
    scales = np.stack([qs, qs[:, half_swap], ks, ks[:, half_swap]], 1)
    w2 = np.zeros((DEPTH, GT * P, P), f)
    w2[:, :GI] = i['L1_ffn_W2']
    arrays = {
        "xT": i['x'].reshape(T, P).T, "cst": cst, "vec": vec,
        "wa": np.concatenate([i['L0_attn_Wq'], i['L0_attn_Wk'], i['L0_attn_Wv']], 1),
        "rel": rel[:, band].transpose(1, 0, 2).reshape(P, -1),
        "ctxT": i['ctx_1024'].transpose(2, 0, 1).reshape(P, -1), "ctxN": i['ctx_1024'],
        "wb": np.concatenate([x[0].T, x[1].T, x[2], x[3], x[3].T, x[4].T, x[5].T], 1),
        "cen": i['L0_ffn_centroids'].T,
        "we1": i['L0_ffn_W1'].transpose(1, 0, 2).reshape(P, -1),
        "we2": i['L0_ffn_W2'].reshape(NE, FT, P, P).transpose(2, 0, 1, 3).reshape(P, -1),
        "wd": np.concatenate([wd, wdo], 1),
        "we": np.concatenate([i['L1_xattn_Wq'].T, i['L1_xattn_Wk'], i['L1_xattn_Wv'].T, i['L1_xattn_Wo'].T], 1),
        "lvec": lvec,
        "wfq": wq,
        "scl": np.broadcast_to(scales.reshape(1, -1), (P, DEPTH * 4 * DH)),
        "wfo": i['L1_ffn_Wo'].reshape(DEPTH, CH, P, P).transpose(0, 2, 1, 3).reshape(DEPTH, P, CH * P),
        "wf1": i['L1_ffn_W1'],
        "wf2": w2.reshape(DEPTH, GT, P, P).transpose(0, 2, 1, 3).reshape(DEPTH, P, GT * P),
    }
    nc = _bacc.Bacc("TRN2", target_bir_lowering=False, num_devices=1)
    given, args = {}, []
    for name, arr in arrays.items():
        arr = np.ascontiguousarray(arr)
        given[f"in_{name}"] = arr
        args.append(nc.dram_tensor(f"in_{name}", arr.shape, _mybir.dt.from_np(arr.dtype), kind="ExternalInput").ap())
    outT = nc.dram_tensor("out_T", (P, T), F32, kind="ExternalOutput").ap()
    decoder(nc, *args, outT)
    r = _run(nc, [given], core_ids=[0])
    return np.ascontiguousarray(r.results[0]["out_T"].T).reshape(NB, SEQ, P)
```

```python
from contextlib import ExitStack

import concourse.bass as bass
from concourse import mybir

F32 = mybir.dt.float32
BF16 = mybir.dt.bfloat16
ACT = mybir.ActivationFunctionType
ALU = mybir.AluOpType
AXX = mybir.AxisListType.X

P = 128
T = 1024
HC = 512
NB = 4
SEQ = 256
EPS = 1e-5
BIG = 3.0e38

AH, ADK = 16, 8
SK = 1601
KT = (SK + P - 1) // P
KLAST = SK - (KT - 1) * P
XSCALE = 1.0 / float(P) ** 0.5
NE, FF = 8, 512
FT = FF // P
NH, DH = 16, 64
CH = NH * DH // P
DEPTH, WIN = 6, 32
GI = 341
GT = 3
QK_SCALE = 8.0
SEGF = P + WIN

V_BQ, V_BK, V_BV, V_HB, V_QB, V_KB, V_CB, V_VB, V_OB, V_LW, V_LB = range(11)
V_EG, V_EB, V_EB2, V_EB1 = 11, 19, 27, 35
NVEC = V_EB1 + NE * FT
L_G, L_B, L_B2, L_B1A, L_B1G = 0, 1, 2, 3, 6
NLV = 9
C_ID, C_MEAN, C_BLK, C_HM, C_PR, C_MD, C_MF, C_ROT = 0, 128, 256, 384, 400, 432, 560, 880
NCST = C_ROT + 4 * 2 * DH


def ln_steps(name, exact):
    return [f"{name}.{s}" for s in ["mean", "xc", "sq", "var", "rs"] + ["rc"] * exact + ["out"]]


def pairs(name, what):
    return [f"{name}.{w}{e}" for w in what for e in ("", "e")]


CHAIN = (ln_steps("A", True) + pairs("A", "qkv") + [f"A.{w}{j}" for j in range(2) for w in ("rc", "on", "ot", "res")]
         + ln_steps("B", True) + pairs("B", "hquws") + ["B.core"] + pairs("B", "cvo")
         + ln_steps("C", True) + ln_steps("C2", False) + ["C.addx"]
         + ["C.lg", "C.mx", "C.eq", "C.pr", "C.m2", "C.oh"] + [f"C.{w}{e}" for e in range(NE) for w in ("bc", "be")]
         + ["C.core"]
         + ln_steps("D", False) + ln_steps("D2", False) + ["D.addx", "D.aff"]
         + ln_steps("E", False) + pairs("E", "qw") + ["E.core"] + pairs("E", "vo")
         + ln_steps("F", False))
AT = {n: i for i, n in enumerate(CHAIN)}
LAYER = (["shift", "v", "core", "wo", "woe", "shift2"] + ln_steps("f", False) + ["aff", "ffn", "w2", "w2e"])
LAT = {n: i for i, n in enumerate(LAYER)}


def decoder(nc, xT, cst, vec, wa, rel, ctxT, ctxN, wb, cen, we1, we2, wd, we, lvec, wfq, scl, wfo, wf1, wf2, out):
    with ExitStack() as ctx:
        def sb(name, cols, dt=F32):
            return ctx.enter_context(nc.sbuf_tensor(name, [P, cols], dt))

        def sem(name):
            return ctx.enter_context(nc.semaphore(name))

        X, XC, SQ, RS, XN, XI = (sb(n, T) for n in ("X", "XC", "SQ", "RS", "XN", "XI"))
        CST = sb("CST", NCST)
        VEC = sb("VEC", NVEC)
        LV = sb("LV", NLV)
        LV6 = sb("LV6", DEPTH * NLV)
        IDB = sb("IDB", P, BF16)
        MDB = sb("MDB", P, BF16)
        MFB = sb("MFB", 2 * SEGF, BF16)
        small = sb("small", 256)
        W_A = sb("W_A", 3 * P)
        W_B = sb("W_B", 7 * P)
        W_E = sb("W_E", 4 * P)
        CEN = sb("CEN", NE)
        MOE = sb("MOE", 2 * NE * FF)
        REL = sb("REL", AH * 3 * P)
        WORK = sb("WORK", 13060 + 11600)

        ident = CST[:, C_ID:C_ID + P]
        mean_w = CST[:, C_MEAN:C_MEAN + P]
        block_w = CST[:, C_BLK:C_BLK + P]
        head_mask = CST[:, C_HM:C_HM + AH]
        prio = CST[:, C_PR:C_PR + 4 * NE].rearrange("p (a e) -> p a e", e=NE)

        def carve(at, cols):
            return WORK[:, at:at + cols], at + cols

        o = 0
        CT, o = carve(o, NB * SK)
        CN, o = carve(o, NB * KT * P)
        ctx_end = o
        CT3 = CT.rearrange("p (b k) -> p b k", b=NB)
        CN4 = CN.rearrange("p (b j d) -> p b j d", b=NB, d=P)
        rel3 = REL[:, :].rearrange("p (h c) -> p h c", h=AH)
        a = ctx_end
        KM, a = carve(a, 2 * AH * SEQ)
        KM4 = KM.rearrange("p (n h k) -> p n h k", n=2, h=AH)
        NS, a = carve(a, 2 * 512)
        PA, a = carve(a, 2 * 512)
        PTA, a = carve(a, 2 * 512)
        NS4 = NS.rearrange("p (n i k) -> p n i k", n=2, i=2)
        PA4 = PA.rearrange("p (n i k) -> p n i k", n=2, i=2)
        PTA4 = PTA.rearrange("p (n j q) -> p n j q", n=2, j=4)
        assert a <= 13060 + 11600
        QA, KA, VA = XI[:, :], SQ[:, :], RS[:, :]
        VA3 = VA.rearrange("p (t d) -> p t d", d=P)
        ON_A = XC[:, 0:512].rearrange("p (n q m) -> p n q m", n=2, q=2)
        a = ctx_end
        XQ, a = carve(a, T)
        XU, a = carve(a, T)
        XW, a = carve(a, T)
        XA, a = carve(a, T)
        PX, a = carve(a, 2 * SK)
        PX3 = PX.rearrange("p (n k) -> p n k", n=2)
        PTX, a = carve(a, 2 * KT * P)
        PTX4 = PTX.rearrange("p (n j q) -> p n j q", n=2, q=P)
        ONX, a = carve(a, 2 * P)
        ONX3 = ONX.rearrange("p (n d) -> p n d", n=2)
        assert a <= 13060 + 11600
        W1M = MOE[:, 0:NE * FF].rearrange("p (e f) -> p e f", e=NE)
        W2M = MOE[:, NE * FF:2 * NE * FF].rearrange("p (e j d) -> p e j d", e=NE, d=P)
        a = ctx_end
        HM, a = carve(a, 2 * FT * HC)
        HM4 = HM.rearrange("p (n j t) -> p n j t", n=2, j=FT)
        XE, a = carve(a, 2 * HC)
        XE3 = XE.rearrange("p (n t) -> p n t", n=2)
        YE, a = carve(a, 2 * HC)
        YE3 = YE.rearrange("p (n t) -> p n t", n=2)
        OHW, a = carve(a, NE * T // 2)
        OH = OHW.bitcast(BF16).rearrange("p (e t) -> p e t", e=NE)
        assert a <= 13060 + 11600
        OHT = small[:, 192:224].bitcast(BF16).rearrange("p (h a e) -> p h a e", h=2, e=NE)
        WDQ = REL[:, 0:3 * NH * DH]
        WDO = REL[:, 3 * NH * DH:3 * NH * DH + CH * P].rearrange("p (c d) -> p c d", c=CH)
        a = ctx_end
        QD, a = carve(a, CH * 256)
        KD, a = carve(a, CH * 256)
        VD, a = carve(a, 4 * NH * (DH + 1))
        OD, a = carve(a, 2 * NH * DH)
        XD, a = carve(a, T)
        XD4 = XD.rearrange("p (n i b) -> p n i b", n=8, i=4)
        assert a <= 13060 + 11600
        QD3, KD3 = (z.rearrange("p (c t) -> p c t", c=CH) for z in (QD, KD))
        VD4 = VD.rearrange("p (n h k) -> p n h k", n=4, k=DH + 1)
        OD3 = OD.rearrange("p (n m) -> p n m", n=2)
        PD4 = SQ[:, :].rearrange("p (n i k) -> p n i k", n=2, i=4)
        PTD4 = XC[:, :].rearrange("p (n i q) -> p n i q", n=2, i=4)
        OTD3 = RS[:, :].rearrange("p (c q) -> p c q", c=CH)
        a = 0
        VF, a = carve(a, 4 * NH * (DH + 1))
        KN, a = carve(a, 4 * NH * DH)
        QN, a = carve(a, 4 * NH * DH)
        QTF, a = carve(a, 2 * SEQ)
        KPF, a = carve(a, 2 * 2 * (SEQ + WIN))
        XSF, a = carve(a, T)
        SQF, a = carve(a, 2 * HC)
        T2F, a = carve(a, 4 * HC)
        PF, a = carve(a, 3 * 512)
        PTF, a = carve(a, 2 * 384)
        GF, a = carve(a, GT * HC)
        YF, a = carve(a, T)
        assert a <= 13060 + 11600, a
        OTF = REL[:, 0:CH * HC].rearrange("p (c t) -> p c t", c=CH)
        ONF = REL[:, CH * HC:CH * HC + 2 * 2 * P].rearrange("p (n q m) -> p n q m", n=2, q=2)
        HF3 = REL[:, CH * HC + 4 * P:CH * HC + 4 * P + GT * HC].rearrange("p (n t) -> p n t", n=GT)
        VF4 = VF.rearrange("p (n h k) -> p n h k", n=4, k=DH + 1)
        KN3, QN3 = (z.rearrange("p (n m) -> p n m", n=4) for z in (KN, QN))
        QTF3 = QTF.rearrange("p (n t) -> p n t", n=2)
        KPF4 = KPF.rearrange("p (n r t) -> p n r t", n=2, r=2)
        SQF3 = SQF.rearrange("p (n t) -> p n t", n=2)
        T2F3 = T2F.rearrange("p (n t) -> p n t", n=4)
        PF3 = PF.rearrange("p (n k) -> p n k", n=3)
        PTF4 = PTF.rearrange("p (n j q) -> p n j q", n=2, j=3)
        GF3 = GF.rearrange("p (n t) -> p n t", n=GT)
        TABF = XN[:, 0:512].rearrange("p (n q d) -> p n q d", n=4, q=2)
        NSQ, NRM, NRC = (XN[:, 512 + 128 * z:640 + 128 * z].rearrange("p (w n h) -> p w n h", w=2, n=4) for z in range(3))
        WFQ = MOE[:, 0:3072]
        WFO = MOE[:, 5120:6144].rearrange("p (c d) -> p c d", c=CH)
        WF1 = MOE[:, 6144:6144 + 2 * GI]
        WF2 = MOE[:, 6144 + 2 * GI:6144 + 2 * GI + GT * P].rearrange("p (j d) -> p j d", j=GT)
        LQ6 = MOE[:, 3072:3072 + DEPTH * 4 * DH]

        PS = [ctx.enter_context(nc.psum_tensor(f"ps{i}", [P, 512], F32)) for i in range(2)]
        PQ = ctx.enter_context(nc.psum_tensor("pq", [P, 4, 512], F32))
        PR = [ctx.enter_context(nc.psum_tensor(f"pr{i}", [P, 512], F32)) for i in range(2)]

        half = [sem("half0"), sem("half1")]
        ld_x, ld_c, ld_v, ld_a, ld_rel, ld_ct, ld_cn, ld_b, ld_moe, ld_d, ld_e = (
            sem(f"ld_{n}") for n in "x cst vec a rel ct cn b moe d e".split())
        cast = sem("cast")
        a_km, a_s, a_ns, a_e, a_t, a_pt, a_o = (sem(f"a_{n}") for n in "km s ns e t pt o".split())
        x_s, x_mx, x_nb1, x_nb2, x_e, x_t, x_pta, x_ptd, x_o, x_rc, x_on, x_ot, x_at = (
            sem(f"x_{n}") for n in "s mx nb1 nb2 e t pta ptd o rc on ot at".split())
        c_xe, c_h, c_r, c_y, c_ye, c_acc = (sem(f"c_{n}") for n in "xe h r y ye acc".split())
        d_p, d_va, d_vd, d_s, d_mx, d_sub, d_e, d_t, d_pt, d_o, d_rc, d_on, d_wo, d_res, d_one = (
            sem(f"d_{n}") for n in "p va vd s mx sub e t pt o rc on wo res one".split())
        f_lv, f_tab, f_qp, f_sq, f_red, f_nrm, f_gd, f_rc1, f_t2, f_t1, f_add, f_km, f_v, f_va, f_cp, f_qt, f_ke = (
            sem(f"f_{n}") for n in "lv tab qp sq red nrm gd rc1 t2 t1 add km v va cp qt ke".split())
        f_s, f_mx, f_sub, f_e, f_t, f_pt, f_o, f_rc, f_on, f_g, f_a, f_ge, f_hh = (
            sem(f"f_{n}") for n in "s mx sub e t pt o rc on g a ge hh".split())
        ld_lv, ld_fq, ld_fo, ld_f1 = (sem(f"ld_{n}") for n in "lv fq fo f1".split())
        stored = sem("stored")

        d_jobs = []
        for u in range(32 + 4):
            d_jobs += [("p", u - 1)] * (1 <= u <= 32) + [("o", u // 4 - 1, g) for g in range(2) if u >= 6 and u % 4 == 2 + g]
        d_job = {j: n for n, j in enumerate(d_jobs)}
        f_jobs = []
        for u in range(32 + 4):
            f_jobs += [("p", u - 2)] * (2 <= u <= 33) + [("o", (u - 4) // 2)] * (u >= 5 and u % 2 == 1)
        f_job = {j: n for n, j in enumerate(f_jobs)}

        block = ctx.enter_context(nc.Block())
        HALVES = range(2)

        def cols(h):
            return slice(h * HC, (h + 1) * HC)

        def at(t, h):
            return t[:, cols(h)] if t.shape[1] == T else t[:, :]

        def turn(eng, h, name):
            if AT[name]:
                eng.wait_ge(half[h], AT[name])

        def ln_pe(pe, name, src, halves=HALVES, turn=turn):
            for h in halves:
                turn(pe, h, f"{name}.mean")
                nc.tensor.matmul(PS[h][:, :], mean_w, at(src, h), start=True, stop=True).then_inc(half[h], 1)
            for h in halves:
                turn(pe, h, f"{name}.var")
                nc.tensor.matmul(PS[h][:, :], mean_w, SQ[:, cols(h)], start=True, stop=True).then_inc(half[h], 1)

        def ln_act(act, name, exact, halves=HALVES, turn=turn):
            for h in halves:
                turn(act, h, f"{name}.sq")
                nc.scalar.activation(SQ[:, cols(h)], XC[:, cols(h)], ACT.Square).then_inc(half[h], 1)
            for h in halves:
                turn(act, h, f"{name}.rs")
                nc.scalar.activation(RS[:, cols(h)], PS[h][:, :], ACT.Sqrt if exact else ACT.Abs_reciprocal_sqrt,
                                     bias=eps_ap).then_inc(half[h], 1)

        def ln_dve(dve, name, src, dst, exact, halves=HALVES, turn=turn):
            for h in halves:
                turn(dve, h, f"{name}.xc")
                nc.vector.tensor_tensor(XC[:, cols(h)], at(src, h), PS[h][:, :], ALU.subtract).then_inc(half[h], 1)
            for h in halves:
                if exact:
                    turn(dve, h, f"{name}.rc")
                    nc.vector.reciprocal(RS[:, cols(h)], RS[:, cols(h)]).then_inc(half[h], 1)
            for h in halves:
                turn(dve, h, f"{name}.out")
                nc.vector.tensor_tensor(at(dst, h), XC[:, cols(h)], RS[:, cols(h)], ALU.mult).then_inc(half[h], 1)

        eps_ap = small[:, 255:256]

        def proj_pe(pe, name, w, src):
            for h in HALVES:
                turn(pe, h, name)
                nc.tensor.matmul(PS[h][:, :], w, src[:, cols(h)], start=True, stop=True).then_inc(half[h], 1)

        def bias_act(act, name, dst, col):
            for h in HALVES:
                turn(act, h, name)
                if col is None:
                    ins = nc.scalar.activation(dst[:, cols(h)], PS[h][:, :], ACT.Copy)
                else:
                    ins = nc.scalar.activation(dst[:, cols(h)], PS[h][:, :], ACT.Identity, bias=VEC[:, col:col + 1])
                ins.then_inc(half[h], 1)

        def add_dve(dve, name, dst, col, other):
            for h in HALVES:
                turn(dve, h, name)
                if col is None:
                    ins = nc.vector.tensor_tensor(dst[:, cols(h)], PS[h][:, :], other[:, cols(h)], ALU.add)
                else:
                    ins = nc.vector.scalar_tensor_tensor(dst[:, cols(h)], PS[h][:, :], VEC[:, col:col + 1],
                                                         other[:, cols(h)], ALU.add, ALU.add)
                ins.then_inc(half[h], 1)

        def x_pe(pe, k, W):
            name = ("B", "E")[k]

            def scores(t):
                b, h = t // 2, t // 4
                n = 8 * k + t
                if t % 4 == 0:
                    turn(pe, h, f"{name}.core")
                if n >= 1:
                    pe.wait_ge(x_e, n)
                for j in range(4):
                    m = min(512, SK - 512 * j)
                    last = nc.tensor.matmul(PQ[:, j, 0:m], W[:, t * P:(t + 1) * P], CT3[:, b, 512 * j:512 * j + m],
                                            start=True, stop=True)
                last.then_inc(x_s, 1)

            def weigh(t):
                b, h, n = t // 2, t // 4, 8 * k + t
                pe.wait_ge(x_e, n + 1)

                def transposed(g):
                    if g == 1:
                        if n:
                            pe.wait_ge(x_ptd, n)
                    elif 3 * n + g:
                        pe.wait_ge(x_pta, (3 * n, 0, 3 * n + 1, 3 * n + 2)[g])
                    for j in range(4 * g, min(4 * g + 4, KT)):
                        rows = P if j < KT - 1 else KLAST
                        last = nc.tensor.transpose(PR[g % 2][0:rows, (j % 4) * P:(j % 4 + 1) * P],
                                                   PX3[:, t % 2, j * P:j * P + rows], ident)
                    last.then_inc(x_t, 1)

                def product(g):
                    if g < 3:
                        pe.wait_ge(x_pta, 3 * n + g + 1)
                    else:
                        pe.wait_ge(x_ptd, n + 1)
                    if g == 0 and n:
                        pe.wait_ge(x_at, n)
                    for j in range(4 * g, min(4 * g + 4, KT)):
                        rows = P if j < KT - 1 else KLAST
                        last = nc.tensor.matmul(PS[h][:, 0:P], PTX4[0:rows, t % 2, j, :], CN4[0:rows, b, j, :],
                                                start=(j == 0), stop=(j == KT - 1))
                    return last

                transposed(0)
                transposed(1)
                transposed(2)
                product(0)
                transposed(3)
                product(1)
                product(2)
                product(3).then_inc(x_o, 1)

            def turn_over(t):
                pe.wait_ge(x_on, 8 * k + t + 1)
                nc.tensor.transpose(PS[t // 4][:, P:2 * P], ONX3[:, t % 2, :], ident).then_inc(x_ot, 1)

            for t in range(8):
                scores(t)
                if t >= 2:
                    turn_over(t - 2)
                if t:
                    weigh(t - 1)
            turn_over(6)
            weigh(7)
            turn_over(7)

        def x_act(act, k):
            def take(u):
                act.wait_ge(x_ot, 8 * k + u + 1)
                nc.scalar.activation(XA[:, u * P:(u + 1) * P], PS[u // 4][:, P:2 * P], ACT.Copy).then_inc(x_at, 1)

            for t in range(9):
                if t >= 2:
                    take(t - 2)
                if t:
                    n = 8 * k + t - 1
                    for g in range(3):
                        act.wait_ge(x_t, 4 * n + g + 1)
                        if n >= 2:
                            act.wait_ge(x_o, n - 1)
                        nc.scalar.activation(PTX4[:, (t - 1) % 2, 4 * g:4 * g + 4, :],
                                             PR[g % 2][:, :].rearrange("p (j q) -> p j q", q=P), ACT.Copy).then_inc(x_pta, 1)
                if t < 8:
                    n = 8 * k + t
                    act.wait_ge(x_nb2, n + 1)
                    if n >= 2:
                        act.wait_ge(x_t, 4 * (n - 1))
                    nc.scalar.activation(PX3[:, t % 2, :], PQ[:, :, :].rearrange("p a b -> p (a b)")[:, 0:SK], ACT.Exp,
                                         bias=small[:, 16 + t:17 + t], scale=XSCALE,
                                         accum_out=small[:, 24 + t:25 + t]).then_inc(x_e, 1)
            take(7)

        def x_dve(dve, k):
            for t in range(9):
                if t < 8:
                    n = 8 * k + t
                    dve.wait_ge(x_s, n + 1)
                    nc.vector.tensor_reduce(small[:, t:t + 1], PQ[:, :, :].rearrange("p a b -> p (a b)")[:, 0:SK],
                                            AXX, ALU.max, negate=True).then_inc(x_mx, 1)
                    dve.wait_ge(x_mx, n + 1)
                    nc.vector.tensor_tensor(small[:, 8 + t:9 + t], small[:, t:t + 1], small[:, 40 + t:41 + t],
                                            ALU.subtract).then_inc(x_nb1, 1)
                    dve.wait_ge(x_nb1, n + 1)
                    nc.vector.tensor_scalar(small[:, 16 + t:17 + t], small[:, 8 + t:9 + t], small[:, 40 + t:41 + t],
                                            XSCALE, ALU.add, ALU.mult).then_inc(x_nb2, 1)
                if t:
                    n, u = 8 * k + t - 1, t - 1
                    dve.wait_ge(x_t, 4 * n + 4)
                    if n >= 2:
                        dve.wait_ge(x_o, n - 1)
                    nc.vector.tensor_copy(PTX4[0:KLAST, u % 2, 12, :], PR[1][0:KLAST, 0:P]).then_inc(x_ptd, 1)
                    dve.wait_ge(x_e, n + 1)
                    nc.vector.reciprocal(small[:, 32 + u:33 + u], small[:, 24 + u:25 + u]).then_inc(x_rc, 1)
                    dve.wait_ge(x_rc, n + 1)
                    dve.wait_ge(x_o, n + 1)
                    if n >= 2:
                        dve.wait_ge(x_ot, n - 1)
                    nc.vector.tensor_scalar(ONX3[:, u % 2, :], PS[u // 4][:, 0:P], small[:, 32 + u:33 + u], None,
                                            ALU.mult).then_inc(x_on, 1)

        def PFS(n):
            return PF3[:, n, :].rearrange("p (q k) -> p q k", q=2)[:, :, 0:SEGF]

        F_BASE = len(CHAIN)
        F_END = F_BASE + DEPTH * len(LAYER)

        def fturn(eng, p, layer, name):
            eng.wait_ge(half[p], layer * len(LAYER) + (F_BASE + LAT[name]))

        KINDS = [(0, 0), (0, 0), (0, 1), (0, 1), (0, 2), (0, 2), (1, 0), (1, 0), (1, 1), (1, 1), (1, 2), (1, 2),
                 (2, 0), (2, 0), (2, 1), (2, 1), (3, 0), (3, 0), (3, 1), (3, 1), (2, 2), (2, 2), (3, 2), (3, 2)]
        SLOTS = len(KINDS)
        ON_POOL = (3, 8, 9, 14, 15, 18, 19)
        TAIL = {"pe": {2: ("wo",), 7: ("f.mean",), 9: ("f.var",), 12: ("ffn0",), 13: ("ffn1",), 15: ("ffn2",), 19: ("w2",)},
                "act": {6: ("f.sq",), 8: ("f.rs",), 12: ("ffn0",), 14: ("ffn1", "ffn2",)},
                "dve": {3: ("woe", "shift2",), 6: ("f.xc",), 8: ("f.out", "aff",), 12: ("ffn0",), 13: ("ffn1",), 14: ("ffn2",), 19: ("w2e",)},
                "pool": {}}

        def copies(p, layer, v):
            return layer * (2 * len(ON_POOL)) + (len(ON_POOL) * p + ON_POOL.index(v) + 1)

        def ffn_banks(p, i):
            return ((PR[0], PR[1]), (PS[1 - p], PR[0]), (PR[1], PS[1 - p]))[i]

        def slot_of(v):
            (n, w), c = KINDS[v], v % 2
            return n, w, c, 2 * n + c if w == 2 else 4 * n + 2 * w + c

        def local_layers(eng, kind, project, core, tail):
            project(0, 0, lambda slot: None)

            def tail_of(p, layer):
                def between(slot):
                    for name in TAIL[kind].get(slot, ()):
                        tail(name, p, layer)
                return between

            with eng.Fori(0, DEPTH - 1) as layer:
                core(0, layer)
                project(1, layer, tail_of(0, layer))
                core(1, layer)
                project(0, layer + 1, tail_of(1, layer))
            core(0, DEPTH - 1)
            project(1, DEPTH - 1, tail_of(0, DEPTH - 1))
            core(1, DEPTH - 1)
            for slot in range(SLOTS):
                tail_of(1, DEPTH - 1)(slot)

        @block.sync
        def _(sp):
            sp.dma_start(X[:, :], xT).then_inc(ld_x, 16)
            sp.dma_start(CST[:, :], cst).then_inc(ld_c, 16)
            sp.dma_start(W_A[:, :], wa).then_inc(ld_a, 16)
            sp.dma_start(VEC[:, :], vec).then_inc(ld_v, 16)
            sp.dma_start(REL[:, :], rel).then_inc(ld_rel, 16)
            sp.dma_start(CT, ctxT).then_inc(ld_ct, 16)
            sp.dma_start(W_B[:, :], wb).then_inc(ld_b, 16)
            for b in range(NB):
                sp.dma_start(CN4[:, b, 0:KT - 1, :], ctxN[b, 0:(KT - 1) * P, :].rearrange("(j p) d -> p j d", p=P)).then_inc(ld_cn, 16)
                sp.dma_start(CN4[0:KLAST, b, KT - 1, :], ctxN[b, (KT - 1) * P:SK, :]).then_inc(ld_cn, 16)
            sp.dma_start(MOE[:, 0:NE * FF], we1).then_inc(ld_moe, 16)
            sp.dma_start(MOE[:, NE * FF:2 * NE * FF], we2).then_inc(ld_moe, 16)
            sp.dma_start(CEN[:, :], cen).then_inc(ld_moe, 16)
            sp.dma_start(W_E[:, :], we).then_inc(ld_e, 16)
            sp.wait_ge(half[1], AT["B.mean"])
            sp.dma_start(REL[:, 0:3 * NH * DH + CH * P], wd).then_inc(ld_d, 16)
            sp.dma_start(LV6[:, :].rearrange("p (l n) -> p l n", l=DEPTH), lvec.rearrange("l p n -> p l n")).then_inc(ld_lv, 16)
            for h in HALVES:
                sp.wait_ge(half[h], AT["C.core"] + 1)
            sp.dma_start(WFQ, wfq[0, :, :]).then_inc(ld_fq, 16)
            sp.dma_start(LQ6, scl).then_inc(ld_fq, 16)
            sp.dma_start(WFO, wfo[0, :, :].rearrange("p (c d) -> p c d", c=CH)).then_inc(ld_fo, 16)
            sp.dma_start(WF1, wf1[0, :, :]).then_inc(ld_f1, 16)
            sp.dma_start(WF2, wf2[0, :, :].rearrange("p (j d) -> p j d", j=GT)).then_inc(ld_f1, 16)
            with sp.Fori(0, DEPTH - 1) as layer:
                fturn(sp, 1, layer, "core")
                sp.dma_start(WFQ, wfq[layer + 1, :, :]).then_inc(ld_fq, 16)
                fturn(sp, 1, layer, "woe")
                sp.dma_start(WFO, wfo[layer + 1, :, :].rearrange("p (c d) -> p c d", c=CH)).then_inc(ld_fo, 16)
                fturn(sp, 1, layer, "w2e")
                sp.dma_start(WF1, wf1[layer + 1, :, :]).then_inc(ld_f1, 16)
                sp.dma_start(WF2, wf2[layer + 1, :, :].rearrange("p (j d) -> p j d", j=GT)).then_inc(ld_f1, 16)
            for h in HALVES:
                sp.wait_ge(half[h], F_END + 1)
            sp.dma_start(out, X[:, :]).then_inc(stored, 16)
            sp.wait_ge(stored, 16)

        @block.gpsimd
        def _(pool):
            pool.wait_ge(ld_c, 16)
            for b in range(NB):
                for h in ((b // 2,) if b % 2 == 0 else ()):
                    pool.wait_ge(half[h], AT["A.ke"] + 1)
                if b >= 2:
                    pool.wait_ge(a_s, 16 * (b - 1))
                nc.gpsimd.tensor_tensor(KM4[:, b % 2, :, :],
                                        KA[:, b * SEQ:(b + 1) * SEQ].unsqueeze(1).to_broadcast([P, AH, SEQ]),
                                        head_mask.unsqueeze(2).to_broadcast([P, AH, SEQ]), ALU.mult).then_inc(a_km, 1)

            def f_project(p, layer, between):
                base = layer * 32 + 16 * p

                def normalise(n):
                    k = KN3[:, n, :].rearrange("p (h k) -> p h k", k=DH)
                    if n % 2 == 0:
                        pool.wait_ge(f_rc1, layer * 4 + (2 * p + n // 2 + 1))
                        pool.wait_ge(f_add, base + (8 * (n // 2) + 6))
                    nc.gpsimd.tensor_tensor(k, k, NRC[:, 0, n, :].unsqueeze(2).to_broadcast([P, NH, DH]), ALU.mult).then_inc(f_km, 1)

                for v in range(SLOTS):
                    n, w, c, i = slot_of(v)
                    if w < 2:
                        t2 = T2F3[:, i % 4, :]
                        if v in ON_POOL:
                            m = copies(p, layer, v)
                            pool.wait_ge(f_cp, m)
                            pool.wait_ge(f_tab, layer + 1)
                            nc.gpsimd.tensor_tensor(t2.rearrange("p (h k) -> p h k", k=DH), t2.rearrange("p (h k) -> p h k", k=DH),
                                                    TABF[:, 2 * (1 - w) + 1, n % 2, :].unsqueeze(1).to_broadcast([P, 8, DH]), ALU.mult).then_inc(f_t2, 1)
                            pool.wait_ge(f_t2, m)
                        dst = (KN3, QN3)[w][:, n, c * 512:(c + 1) * 512]
                        pool.wait_ge(f_t1, base + (i + 1))
                        nc.gpsimd.tensor_tensor(dst, dst, t2, ALU.add).then_inc(f_add, 1)
                    if v in (14, 16):
                        normalise(int(v == 16))
                normalise(2)
                normalise(3)

            local_layers(pool, "pool", f_project, lambda p, layer: None, lambda name, p, layer: None)

        @block.tensor
        def _(pe):
            pe.wait_ge(ld_x, 16)
            pe.wait_ge(ld_c, 16)
            ln_pe(pe, "A", X)
            pe.wait_ge(ld_a, 16)
            proj_pe(pe, "A.q", W_A[:, 0:P], XN)
            proj_pe(pe, "A.k", W_A[:, P:2 * P], XN)
            for h in HALVES:
                turn(pe, h, "A.v")
                for t in range(4):
                    last = nc.tensor.matmul(PS[h][:, t * P:(t + 1) * P], XN[:, h * HC + t * P:h * HC + (t + 1) * P],
                                            W_A[:, 2 * P:3 * P], start=True, stop=True)
                last.then_inc(half[h], 1)

            def a_scores(u):
                b, hp, q = u // 16, u // 2 % 8, u % 2
                if u % 16 == 0:
                    pe.wait_ge(half[b // 2], AT["A.ve"] + 1)
                    pe.wait_ge(a_km, b + 1)
                if u >= 2:
                    pe.wait_ge(a_ns, u - 1)
                nc.tensor.matmul(PQ[:, u % 2, :], QA[:, (2 * b + q) * P:(2 * b + q + 1) * P],
                                 KM4[:, b % 2, 2 * hp:2 * hp + 2, :], start=True, stop=True).then_inc(a_s, 1)

            def a_transpose(u):
                pe.wait_ge(a_e, u + 1)
                if u >= 2:
                    pe.wait_ge(a_pt, u - 1)
                for i in range(2):
                    for k in range(2):
                        last = nc.tensor.transpose(PR[u % 2][:, (2 * i + k) * P:(2 * i + k + 1) * P],
                                                   PA4[:, u % 2, i, k * P:(k + 1) * P], ident)
                last.then_inc(a_t, 1)

            def a_weigh(u):
                b, hp, q = u // 16, u // 2 % 8, u % 2
                pe.wait_ge(a_pt, u + 1)
                if u % 16 == 0 and b >= 2:
                    pe.wait_ge(half[(b - 2) // 2], AT[f"A.on{b % 2}"] + 1)
                for i in range(2):
                    c = q * P + (2 * hp + i) * ADK
                    for k in range(2):
                        last = nc.tensor.matmul(PQ[:, 2 + b % 2, c:c + ADK], PTA4[:, u % 2, 2 * i + k, :],
                                                VA3[:, 2 * b + k, (2 * hp + i) * ADK:(2 * hp + i + 1) * ADK],
                                                start=(k == 0), stop=(k == 1))
                last.then_inc(a_o, 1)

            def a_out(b):
                turn(pe, b // 2, f"A.ot{b % 2}")
                for q in range(2):
                    last = nc.tensor.transpose(PS[b // 2][:, q * P:(q + 1) * P], ON_A[:, b % 2, q, :], ident)
                last.then_inc(half[b // 2], 1)

            for u in range(64 + 2):
                if u < 64:
                    a_scores(u)
                if 0 <= u - 1 < 64:
                    a_transpose(u - 1)
                if u >= 2 and u - 2 < 64:
                    a_weigh(u - 2)
                if u >= 19 and (u - 19) % 16 == 0:
                    a_out((u - 19) // 16)
            a_out(3)

            ln_pe(pe, "B", X)
            pe.wait_ge(ld_b, 16)
            pe.wait_ge(ld_v, 16)
            proj_pe(pe, "B.h", W_B[:, 0:P], XN)
            proj_pe(pe, "B.q", W_B[:, P:2 * P], XI)
            proj_pe(pe, "B.u", W_B[:, 2 * P:3 * P], XQ)
            proj_pe(pe, "B.w", W_B[:, 3 * P:4 * P], XU)
            for h in HALVES:
                turn(pe, h, "B.s")
                for t in range(4):
                    c = h * HC + t * P
                    nc.tensor.matmul(PS[h][:, t:t + 1], XQ[:, c:c + P], VEC[:, V_KB:V_KB + 1], start=True, stop=False)
                    last = nc.tensor.matmul(PS[h][:, t:t + 1], XU[:, c:c + P], VEC[:, V_CB:V_CB + 1], start=False, stop=True)
                last.then_inc(half[h], 1)
            pe.wait_ge(ld_ct, 16)
            pe.wait_ge(ld_cn, 16 * 2 * NB)
            x_pe(pe, 0, XW)
            proj_pe(pe, "B.c", W_B[:, 4 * P:5 * P], XA)
            proj_pe(pe, "B.v", W_B[:, 5 * P:6 * P], XI)
            proj_pe(pe, "B.o", W_B[:, 6 * P:7 * P], XI)

            ln_pe(pe, "C", X)
            ln_pe(pe, "C2", XN)
            pe.wait_ge(ld_moe, 48)
            for h in HALVES:
                turn(pe, h, "C.lg")
                for t in range(4):
                    last = nc.tensor.matmul(PS[h][:, t * NE:(t + 1) * NE], XN[:, h * HC + t * P:h * HC + (t + 1) * P],
                                            CEN[:, :], start=True, stop=True)
                last.then_inc(half[h], 1)
            for e in range(NE):
                for h in HALVES:
                    turn(pe, h, f"C.bc{e}")
                    for t in range(4):
                        last = nc.tensor.matmul(PS[h][:, t * P:(t + 1) * P], OHT[:, h, t, e:e + 1].to_broadcast([P, P]),
                                                IDB[:, :], start=True, stop=True)
                    last.then_inc(half[h], 1)

            def w2(u):
                e = u // 2
                pe.wait_ge(c_r, 4 * u + 4)
                if u >= 2:
                    pe.wait_ge(c_ye, u - 1)
                for j in range(FT):
                    last = nc.tensor.matmul(PR[u % 2][:, :], W2M[:, e, j, :], HM4[:, u % 2, j, :], start=(j == 0), stop=(j == FT - 1))
                last.then_inc(c_y, 1)

            for u in range(2 * NE):
                e = u // 2
                pe.wait_ge(c_xe, u + 1)
                for j in range(FT):
                    if u:
                        pe.wait_ge(c_r, 4 * (u - 1) + j + 1)
                    nc.tensor.matmul(PQ[:, j, :], W1M[:, e, j * P:(j + 1) * P], XE3[:, u % 2, :], start=True, stop=True).then_inc(c_h, 1)
                if u:
                    w2(u - 1)
            w2(2 * NE - 1)

            ln_pe(pe, "D", X)
            ln_pe(pe, "D2", XN)
            pe.wait_ge(ld_d, 16)

            def d_project(g):
                if g == 0:
                    for h in HALVES:
                        turn(pe, h, "E.mean")
                for w in range(12):
                    n = 12 * g + w
                    bank = PQ[:, 2 + n % 2, :]
                    if w == 0 and g >= 2:
                        pe.wait_ge(d_res, 2 * g - 2)
                    if n >= 2:
                        pe.wait_ge(d_va if n % 2 == 0 else d_vd, n // 2)
                    if w < 8:
                        for k in range(2):
                            c = 2 * (w // 2) + k + (w % 2) * CH
                            last = nc.tensor.matmul(bank[:, k * 256:(k + 1) * 256], WDQ[:, c * P:(c + 1) * P],
                                                    XD[:, 256 * g:256 * (g + 1)], start=True, stop=True)
                    else:
                        b0 = 256 * g + P * ((w - 8) // 2)
                        last = nc.tensor.matmul(bank, XD[:, b0:b0 + P],
                                                WDQ[:, 2 * NH * DH + 512 * (w % 2):2 * NH * DH + 512 * (w % 2) + 512],
                                                start=True, stop=True)
                    last.then_inc(d_p, 1)

            for u in range(32 + 5):
                if u < 32:
                    g, n, q = u // 8, u // 4, u % 4
                    if u % 8 == 0:
                        d_project(g)
                        pe.wait_ge(d_va, 6 * (g + 1))
                        pe.wait_ge(d_vd, 6 * (g + 1))
                    if u >= 2:
                        pe.wait_ge(d_sub, u - 1)
                    nc.tensor.matmul(PQ[:, u % 2, :], IDB[:, :], MDB[:, :].unsqueeze(1).to_broadcast([P, 4, P]),
                                     start=True, stop=False)
                    for i in range(4):
                        r, c, b0 = 64 * (q % 2), 4 * (q // 2) + i, P * (n % 2)
                        last = nc.tensor.matmul(PQ[:, u % 2, i * P:(i + 1) * P], QD3[r:r + 64, c, b0:b0 + P],
                                                KD3[r:r + 64, c, b0:b0 + P], start=False, stop=(i == 3))
                    last.then_inc(d_s, 1)
                if 0 <= u - 1 < 32:
                    v = u - 1
                    job = d_job["p", v]
                    pe.wait_ge(d_e, v + 1)
                    if job >= 2:
                        pe.wait_ge(d_pt, job - 1)
                    for i in range(4):
                        last = nc.tensor.transpose(PR[job % 2][:, i * P:(i + 1) * P], PD4[:, v % 2, i, :], ident)
                    last.then_inc(d_t, 1)
                if 0 <= u - 2 < 32:
                    v = u - 2
                    pe.wait_ge(d_pt, d_job["p", v] + 1)
                    if v >= 2:
                        pe.wait_ge(d_on, v - 1)
                    for i in range(4):
                        last = nc.tensor.matmul(PS[v % 2][:, i * (DH + 1):(i + 1) * (DH + 1)], PTD4[:, v % 2, i, :],
                                                VD4[:, v // 4 % 4, 2 * (4 * (v % 4 // 2) + i) + v % 2, :], start=True, stop=True)
                    last.then_inc(d_o, 1)
                if 6 <= u < 36 and u % 4 >= 2:
                    n, g = u // 4 - 1, u % 4 - 2
                    job = d_job["o", n, g]
                    pe.wait_ge(d_on, 4 * n + 4)
                    pe.wait_ge(d_pt, job - 1)
                    for i in range(4):
                        c = 4 * g + i
                        last = nc.tensor.transpose(PR[job % 2][:, i * P:(i + 1) * P], OD3[:, n % 2, c * P:(c + 1) * P], ident)
                    last.then_inc(d_t, 1)
                if u >= 8 and u % 4 == 0:
                    n = u // 4 - 2
                    pe.wait_ge(d_pt, d_job["o", n, 1] + 1)
                    if n >= 2:
                        pe.wait_ge(d_res, n - 1)
                    for h in (d_va, d_vd):
                        pe.wait_ge(h, 6 * (min(u, 31) // 8 + 1))
                    for c in range(CH):
                        last = nc.tensor.matmul(PQ[:, 2 + n % 2, 0:P], WDO[:, c, :], OTD3[:, c, :], start=(c == 0), stop=(c == CH - 1))
                    last.then_inc(d_wo, 1)

            pe.wait_ge(d_res, 8)
            ln_pe(pe, "E", X)
            pe.wait_ge(ld_e, 16)
            proj_pe(pe, "E.q", W_E[:, 0:P], XN)
            proj_pe(pe, "E.w", W_E[:, P:2 * P], XQ)
            x_pe(pe, 1, XW)
            proj_pe(pe, "E.v", W_E[:, 2 * P:3 * P], XA)
            proj_pe(pe, "E.o", W_E[:, 3 * P:4 * P], XI)
            ln_pe(pe, "F", X)

            def f_project(p, layer, between):
                fturn(pe, p, layer, "v")
                pe.wait_ge(ld_fq, layer * 16 + 32)
                for v in range(SLOTS):
                    n, w, c, i = slot_of(v)
                    if v >= 4:
                        _, w4, _, i4 = slot_of(v - 4)
                        if w4 == 2:
                            pe.wait_ge(f_va, layer * 16 + (8 * p + i4 + 1))
                        else:
                            pe.wait_ge(f_t1, layer * 32 + (16 * p + i4 + 1))
                            if v - 4 in ON_POOL:
                                pe.wait_ge(f_cp, copies(p, layer, v - 4))
                    w0 = (1, 0, 2)[w] * NH * DH + c * 512
                    nc.tensor.matmul(PQ[:, v % 4, :], XSF[:, p * HC + n * P:p * HC + (n + 1) * P], WFQ[:, w0:w0 + 512],
                                     start=True, stop=True).then_inc(f_v if w == 2 else f_qp, 1)
                    between(v)

            def f_core(p, layer):
                base = layer * 64 + 32 * p
                jbase = layer * 96 + 48 * p
                kbase = layer * 32 + 16 * p
                pe.wait_ge(f_va, layer * 16 + (8 * p + 8))

                def transpose_qk(k):
                    j, c = k // 8, k % 8
                    pe.wait_ge(f_km, layer * 8 + (4 * p + 2 * j + 2))
                    if c == 0:
                        pe.wait_ge(f_add, layer * 32 + (16 * p + 8 * j + 8))
                    if k:
                        pe.wait_ge(f_ke, kbase + k)
                    for i, src in enumerate((QN3, QN3, KN3, KN3)):
                        last = nc.tensor.transpose(PS[p][:, i * P:(i + 1) * P], src[:, 2 * j + i % 2, c * P:(c + 1) * P], ident)
                    last.then_inc(f_qt, 1)

                transpose_qk(0)
                for u in range(32 + 4):
                    if u < 32:
                        k = u // 2
                        if u % 2 == 0 and k + 1 < 16:
                            transpose_qk(k + 1)
                        pe.wait_ge(f_ke, kbase + (k + 1))
                        if u >= 2:
                            pe.wait_ge(f_sub, base + (u - 1))
                        nc.tensor.matmul(PQ[:, u % 2, 0:2 * SEGF], IDB[:, :], MFB[:, :], start=True, stop=False)
                        for q in range(2):
                            last = nc.tensor.matmul(PQ[:, u % 2, q * SEGF:(q + 1) * SEGF], QTF3[:, k % 2, q * P:(q + 1) * P],
                                                    KPF4[:, k % 2, u % 2, q * P:q * P + SEGF], start=False, stop=(q == 1))
                        last.then_inc(f_s, 1)
                    if 0 <= u - 2 < 32:
                        v = u - 2
                        job = f_job["p", v]
                        pe.wait_ge(f_e, base + (v + 1))
                        if job >= 2:
                            pe.wait_ge(f_pt, jbase + (job - 1))
                        for i in range(3):
                            last = nc.tensor.transpose(PR[job % 2][:, i * P:(i + 1) * P],
                                                       PF3[:, v % 3, WIN + i * P:WIN + (i + 1) * P], ident)
                        last.then_inc(f_t, 1)
                    if 0 <= u - 3 < 32:
                        v = u - 3
                        j, h, k = v // 16, v % 16, v // 2
                        pe.wait_ge(f_pt, jbase + (f_job["p", v] + 1))
                        if v % 2 == 0 and k >= 2:
                            pe.wait_ge(f_on, kbase + (k - 1))
                        o = PQ[:, 2 + k % 2, :]
                        for q, i, kt in ((0, 0, 0), (1, 1, 0), (1, 2, 1)):
                            c = (2 * q + h % 2) * (DH + 1)
                            last = nc.tensor.matmul(o[:, c:c + DH + 1], PTF4[:, v % 2, i, :], VF4[:, 2 * j + kt, h, :],
                                                    start=(i < 2), stop=(i != 1))
                        last.then_inc(f_o, 1)
                    if u >= 5 and u % 2 == 1:
                        k = (u - 4) // 2
                        job = f_job["o", k]
                        pe.wait_ge(f_on, kbase + (k + 1))
                        pe.wait_ge(f_pt, jbase + (job - 1))
                        for q in range(2):
                            last = nc.tensor.transpose(PR[job % 2][:, q * P:(q + 1) * P], ONF[:, k % 2, q, :], ident)
                        last.then_inc(f_t, 1)

            def f_tail(name, p, layer):
                xs = XSF[:, cols(p)]
                if name == "wo":
                    fturn(pe, p, layer, "wo")
                    pe.wait_ge(f_pt, layer * 96 + (48 * p + 48))
                    pe.wait_ge(ld_fo, layer * 16 + 16)
                    for c in range(CH):
                        last = nc.tensor.matmul(PS[p][:, :], WFO[:, c, :], OTF[:, c, :], start=(c == 0), stop=(c == CH - 1))
                    last.then_inc(half[p], 1)
                elif name in ("f.mean", "f.var"):
                    fturn(pe, p, layer, name)
                    src = xs if name == "f.mean" else SQ[:, cols(p)]
                    nc.tensor.matmul(PS[p][:, :], mean_w, src, start=True, stop=True).then_inc(half[p], 1)
                elif name.startswith("ffn"):
                    i = int(name[3])
                    m = min(P, GI - i * P)
                    gate, value = ffn_banks(p, i)
                    if i == 0:
                        fturn(pe, p, layer, "ffn")
                        pe.wait_ge(ld_f1, layer * 32 + 32)
                    if i == 2:
                        pe.wait_ge(f_hh, layer * 6 + (3 * p + 1))
                    nc.tensor.matmul(gate[0:m, :], WF1[:, GI + i * P:GI + i * P + m], xs, start=True, stop=True).then_inc(f_g, 1)
                    if i:
                        pe.wait_ge(f_ge, layer * 6 + (3 * p + i))
                    nc.tensor.matmul(value[0:m, :], WF1[:, i * P:i * P + m], xs, start=True, stop=True).then_inc(f_a, 1)
                elif name == "w2":
                    fturn(pe, p, layer, "w2")
                    for i in range(GT):
                        m = min(P, GI - i * P)
                        last = nc.tensor.matmul(PS[p][:, :], WF2[0:m, i, :], HF3[0:m, i, :], start=(i == 0), stop=(i == GT - 1))
                    last.then_inc(half[p], 1)

            local_layers(pe, "pe", f_project, f_core, f_tail)

        @block.scalar
        def _(act):
            act.wait_ge(cast, 2)
            ln_act(act, "A", True)
            act.wait_ge(ld_v, 16)
            bias_act(act, "A.ke", KA, V_BK)
            bias_act(act, "A.ve", VA, None)
            for u in range(64):
                q = u % 2
                act.wait_ge(a_ns, u + 1)
                if u >= 2:
                    act.wait_ge(a_t, u - 1)
                for i in range(2):
                    h = 2 * (u // 2 % 8) + i
                    c = 64 + (u // 16 % 2) * 32 + q * AH + h
                    last = nc.scalar.activation(PA4[:, u % 2, i, :], NS4[:, u % 2, i, :], ACT.Exp, scale=-1.0,
                                                bias=small[:, 240 + 2 * (u % 4) + i:241 + 2 * (u % 4) + i],
                                                accum_out=small[:, c:c + 1])
                last.then_inc(a_e, 1)
            ln_act(act, "B", True)
            bias_act(act, "B.he", XI, V_HB)
            bias_act(act, "B.qe", XQ, V_QB)
            bias_act(act, "B.ue", XU, None)
            bias_act(act, "B.we", XW, None)
            x_act(act, 0)
            bias_act(act, "B.ce", XI, V_CB)
            ln_act(act, "C", True)
            ln_act(act, "C2", False)
            for e in range(NE):
                for h in HALVES:
                    turn(act, h, f"C.be{e}")
                    nc.scalar.activation(OH[:, e, cols(h)], PS[h][:, :], ACT.Copy).then_inc(half[h], 1)
            for u in range(2 * NE):
                for j in range(FT):
                    act.wait_ge(c_h, 4 * u + j + 1)
                    if u >= 2:
                        act.wait_ge(c_y, u - 1)
                    k = V_EB1 + (u // 2) * FT + j
                    nc.scalar.activation(HM4[:, u % 2, j, :], PQ[:, j, :], ACT.Relu, bias=VEC[:, k:k + 1]).then_inc(c_r, 1)

            ln_act(act, "D", False)
            ln_act(act, "D2", False)

            def d_evac(g):
                for w in range(0, 12, 2):
                    act.wait_ge(d_p, 12 * g + w + 1)
                    if w < 8:
                        dst = QD3[:, w:w + 2, :].rearrange("p c t -> p (c t)")
                        src = PQ[:, 2, :]
                    else:
                        dst = VD4[:, (2 * g + (w - 8) // 2) % 4, 0:8, 0:DH]
                        src = PQ[:, 2, :].rearrange("p (h k) -> p h k", k=DH)
                    nc.scalar.activation(dst, src, ACT.Copy).then_inc(d_va, 1)

            act.wait_ge(d_one, 1)
            for u in range(32 + 4):
                if u < 32 and u % 8 == 0:
                    d_evac(u // 8)
                if 0 <= u - 1 < 32:
                    v = u - 1
                    job = d_job["p", v]
                    act.wait_ge(d_t, job + 1)
                    if v >= 2:
                        act.wait_ge(d_o, v - 1)
                    nc.scalar.activation(PTD4[:, v % 2, :, :], PR[job % 2][:, :].rearrange("p (i q) -> p i q", i=4),
                                         ACT.Copy).then_inc(d_pt, 1)
                if u < 32:
                    act.wait_ge(d_sub, u + 1)
                    nc.scalar.activation(PD4[:, u % 2, :, :], PD4[:, u % 2, :, :], ACT.Exp, scale=XSCALE).then_inc(d_e, 1)
                if u >= 6 and u % 4 >= 2:
                    n, g = u // 4 - 1, u % 4 - 2
                    job = d_job["o", n, g]
                    act.wait_ge(d_t, job + 1)
                    if n:
                        act.wait_ge(d_wo, n)
                    nc.scalar.activation(OTD3[:, 4 * g:4 * g + 4, :], PR[job % 2][:, :].rearrange("p (i q) -> p i q", i=4),
                                         ACT.Copy).then_inc(d_pt, 1)

            ln_act(act, "E", False)
            bias_act(act, "E.qe", XQ, None)
            bias_act(act, "E.we", XW, None)
            x_act(act, 1)
            bias_act(act, "E.ve", XI, None)
            ln_act(act, "F", False)

            def f_project(p, layer, between):
                base = layer * 32 + 16 * p

                def norms(j):
                    act.wait_ge(f_red, base + 8 * (j + 1))
                    nc.scalar.activation(NRM[:, :, 2 * j:2 * j + 2, :], NSQ[:, :, 2 * j:2 * j + 2, :], ACT.Sqrt).then_inc(f_nrm, 1)

                for v in range(SLOTS):
                    n, w, c, i = slot_of(v)
                    if w == 2:
                        act.wait_ge(f_v, layer * 16 + (8 * p + i + 1))
                        nc.scalar.activation(VF4[:, n, 8 * c:8 * c + 8, 0:DH], PQ[:, v % 4, :].rearrange("p (h k) -> p h k", k=DH),
                                             ACT.Copy).then_inc(f_va, 1)
                    else:
                        act.wait_ge(f_qp, base + (i + 1))
                        if i >= 2:
                            act.wait_ge(f_red, base + (i - 1))
                        nc.scalar.activation(SQF3[:, i % 2, :], PQ[:, v % 4, :], ACT.Square).then_inc(f_sq, 1)
                        if v in ON_POOL:
                            if i >= 4:
                                act.wait_ge(f_add, base + (i - 3))
                            nc.scalar.activation(T2F3[:, i % 4, :].rearrange("p (h s k) -> p h s k", s=2, k=DH // 2),
                                                 PQ[:, v % 4, :].rearrange("p (h s k) -> p h s k", s=2, k=DH // 2)[:, :, ::-1, :],
                                                 ACT.Copy).then_inc(f_cp, 1)
                    if v == 9:
                        norms(0)
                    if v == 20:
                        norms(1)
                    between(v)

            def f_core(p, layer):
                base = layer * 64 + 32 * p
                jbase = layer * 96 + 48 * p
                kbase = layer * 32 + 16 * p

                def take_qk(k):
                    act.wait_ge(f_qt, kbase + (k + 1))
                    if k >= 2:
                        act.wait_ge(f_s, base + (2 * k - 2))
                    nc.scalar.activation(QTF3[:, k % 2, :], PS[p][:, 0:SEQ], ACT.Copy)
                    for r in range(2):
                        rows = slice(64 * r, 64 * r + 64)
                        last = nc.scalar.activation(KPF4[rows, k % 2, r, WIN:WIN + SEQ], PS[p][rows, SEQ:2 * SEQ], ACT.Copy)
                    last.then_inc(f_ke, 1)

                take_qk(0)
                for u in range(32 + 4):
                    if u < 32 and u % 2 == 0 and u // 2 + 1 < 16:
                        take_qk(u // 2 + 1)
                    if 0 <= u - 2 < 32:
                        v = u - 2
                        job = f_job["p", v]
                        act.wait_ge(f_t, jbase + (job + 1))
                        if v >= 2:
                            act.wait_ge(f_o, base + (v - 1))
                        nc.scalar.activation(PTF4[:, v % 2, :, :], PR[job % 2][:, 0:3 * P].rearrange("p (i q) -> p i q", i=3),
                                             ACT.Copy).then_inc(f_pt, 1)
                    if u < 32:
                        act.wait_ge(f_sub, base + (u + 1))
                        nc.scalar.activation(PFS(u % 3), PFS(u % 3), ACT.Exp, scale=QK_SCALE).then_inc(f_e, 1)
                    if u >= 5 and u % 2 == 1:
                        k = (u - 4) // 2
                        job = f_job["o", k]
                        act.wait_ge(f_t, jbase + (job + 1))
                        nc.scalar.activation(OTF[:, k % 8, (k // 8) * SEQ:(k // 8 + 1) * SEQ], PR[job % 2][:, 0:SEQ],
                                             ACT.Copy).then_inc(f_pt, 1)

            def f_tail(name, p, layer):
                if name == "f.sq":
                    fturn(act, p, layer, name)
                    nc.scalar.activation(SQ[:, cols(p)], XC[:, cols(p)], ACT.Square).then_inc(half[p], 1)
                elif name == "f.rs":
                    fturn(act, p, layer, name)
                    nc.scalar.activation(RS[:, cols(p)], PS[p][:, :], ACT.Abs_reciprocal_sqrt, bias=eps_ap).then_inc(half[p], 1)
                elif name.startswith("ffn"):
                    i = int(name[3])
                    m = min(P, GI - i * P)
                    act.wait_ge(f_g, layer * 6 + (3 * p + i + 1))
                    nc.scalar.activation(GF3[0:m, i, :], ffn_banks(p, i)[0][0:m, :], ACT.Gelu, bias=LV[0:m, L_B1G + i:L_B1G + i + 1]).then_inc(f_ge, 1)

            local_layers(act, "act", f_project, f_core, f_tail)

        @block.vector
        def _(dve):
            dve.wait_ge(ld_c, 16)
            nc.vector.tensor_copy(IDB[:, :], ident).then_inc(cast, 1)
            nc.vector.memset(small[:, 224:256], EPS).then_inc(cast, 1)
            nc.vector.memset(small[:, 0:192], 0.0).then_inc(cast, 1)
            nc.vector.tensor_copy(MDB[:, :], CST[:, C_MD:C_MD + P]).then_inc(cast, 1)
            nc.vector.tensor_copy(MFB[:, :], CST[:, C_MF:C_MF + 2 * SEGF]).then_inc(cast, 1)
            dve.wait_ge(cast, 3)
            ln_dve(dve, "A", X, XN, True)
            dve.wait_ge(ld_v, 16)
            for h in HALVES:
                turn(dve, h, "A.qe")
                nc.vector.tensor_scalar(QA[:, cols(h)], PS[h][:, :], VEC[:, V_BQ:V_BQ + 1], ADK ** -0.5,
                                        ALU.add, ALU.mult).then_inc(half[h], 1)
            dve.wait_ge(ld_rel, 16)

            def a_out(b):
                h, j = b // 2, b % 2
                r = small[:, 128 + 32 * j:160 + 32 * j]
                turn(dve, h, f"A.rc{j}")
                dve.wait_ge(a_e, 16 * (b + 1))
                nc.vector.reciprocal(r, small[:, 64 + 32 * j:96 + 32 * j]).then_inc(half[h], 1)
                turn(dve, h, f"A.on{j}")
                dve.wait_ge(a_o, 16 * (b + 1))
                nc.vector.tensor_tensor(ON_A[:, j, :, :].rearrange("p q (h k) -> p (q h) k", k=ADK),
                                        PQ[:, 2 + j, 0:2 * P].rearrange("p (x k) -> p x k", k=ADK),
                                        r.unsqueeze(2).to_broadcast([P, 2 * AH, ADK]), ALU.mult).then_inc(half[h], 1)

            def a_residual(b):
                h, j = b // 2, b % 2
                turn(dve, h, f"A.res{j}")
                x = X[:, b * SEQ:(b + 1) * SEQ]
                nc.vector.scalar_tensor_tensor(x, PS[h][:, 0:SEQ], VEC[:, V_BV:V_BV + 1], x, ALU.add, ALU.add).then_inc(half[h], 1)

            for u in range(64 + 2):
                if u < 64:
                    q = u % 2
                    dve.wait_ge(a_s, u + 1)
                    if u >= 2:
                        dve.wait_ge(a_e, u - 1)
                    for i in range(2):
                        h = 2 * (u // 2 % 8) + i
                        last = nc.vector.tensor_tensor_reduce(
                            out=NS4[:, u % 2, i, :], in0=PQ[:, u % 2, i * SEQ:(i + 1) * SEQ],
                            in1=rel3[:, h, P - q * P:P - q * P + SEQ], scale=-1.0, scalar=BIG,
                            op0=ALU.add, op1=ALU.min, accum_out=small[:, 240 + 2 * (u % 4) + i:241 + 2 * (u % 4) + i])
                    last.then_inc(a_ns, 1)
                if u >= 1 and u - 1 < 64:
                    v = u - 1
                    dve.wait_ge(a_t, v + 1)
                    if v >= 2:
                        dve.wait_ge(a_o, v - 1)
                    nc.vector.tensor_copy(PTA4[:, v % 2, :, :], PR[v % 2][:, :].rearrange("p (j q) -> p j q", j=4)).then_inc(a_pt, 1)
                if u >= 18 and (u - 18) % 16 == 0:
                    a_out((u - 18) // 16)
                if u >= 20 and (u - 20) % 16 == 0:
                    a_residual((u - 20) // 16)
            a_out(3)
            a_residual(3)

            ln_dve(dve, "B", X, XN, True)
            for h in HALVES:
                turn(dve, h, "B.se")
                nc.vector.tensor_copy(small[:, 40 + 4 * h:44 + 4 * h], PS[h][:, 0:4]).then_inc(half[h], 1)
            x_dve(dve, 0)
            for h in HALVES:
                turn(dve, h, "B.core")
                dve.wait_ge(x_at, 4 * (h + 1))
                nc.vector.memset(small[:, 48 + h:49 + h], 0.0).then_inc(half[h], 1)
            add_dve(dve, "B.ve", XI, V_VB, XQ)
            add_dve(dve, "B.oe", X, V_OB, X)

            ln_dve(dve, "C", X, XN, True)
            ln_dve(dve, "C2", XN, XI, False)
            for h in HALVES:
                turn(dve, h, "C.addx")
                nc.vector.tensor_tensor(X[:, cols(h)], X[:, cols(h)], XN[:, cols(h)], ALU.add).then_inc(half[h], 1)
            for h in HALVES:
                lg = small[:, 64 + 32 * h:96 + 32 * h].rearrange("p (a e) -> p a e", e=NE)
                mx = small[:, 128 + 8 * h:132 + 8 * h]
                m2 = small[:, 132 + 8 * h:136 + 8 * h]
                ps = PS[h][:, 0:32].rearrange("p (a e) -> p a e", e=NE)
                turn(dve, h, "C.mx")
                nc.vector.tensor_reduce(mx, ps, AXX, ALU.max).then_inc(half[h], 1)
                turn(dve, h, "C.eq")
                nc.vector.tensor_tensor(lg, ps, mx.unsqueeze(2).to_broadcast([P, 4, NE]), ALU.is_equal).then_inc(half[h], 1)
                turn(dve, h, "C.pr")
                nc.vector.tensor_tensor(lg, lg, prio, ALU.mult).then_inc(half[h], 1)
                turn(dve, h, "C.m2")
                nc.vector.tensor_reduce(m2, lg, AXX, ALU.max).then_inc(half[h], 1)
                turn(dve, h, "C.oh")
                nc.vector.tensor_tensor(OHT[:, h, :, :], lg, m2.unsqueeze(2).to_broadcast([P, 4, NE]), ALU.is_equal).then_inc(half[h], 1)

            def expert_in(u):
                e, h = u // 2, u % 2
                if u < 2:
                    dve.wait_ge(half[h], AT["C.core"])
                else:
                    dve.wait_ge(c_h, 4 * (u - 1))
                nc.vector.tensor_scalar(XE3[:, u % 2, :], XI[:, cols(h)], VEC[:, V_EG + e:V_EG + e + 1],
                                        VEC[:, V_EB + e:V_EB + e + 1], ALU.mult, ALU.add).then_inc(c_xe, 1)

            expert_in(0)
            expert_in(1)
            for u in range(2 * NE):
                e, h = u // 2, u % 2
                if u + 2 < 2 * NE:
                    expert_in(u + 2)
                dve.wait_ge(c_y, u + 1)
                if u >= 2:
                    dve.wait_ge(c_acc, u - 1)
                nc.vector.scalar_tensor_tensor(YE3[:, u % 2, :], PR[u % 2][:, :], VEC[:, V_EB2 + e:V_EB2 + e + 1],
                                               OH[:, e, cols(h)], ALU.add, ALU.mult).then_inc(c_ye, 1)
                dve.wait_ge(c_ye, u + 1)
                nc.vector.tensor_tensor(X[:, cols(h)], X[:, cols(h)], YE3[:, u % 2, :], ALU.add).then_inc(c_acc, 1)
            for h in HALVES:
                dve.wait_ge(c_acc, 2 * NE)
                turn(dve, h, "C.core")
                nc.vector.memset(small[:, 48 + h:49 + h], 0.0).then_inc(half[h], 1)

            ln_dve(dve, "D", X, XN, False)
            ln_dve(dve, "D2", XN, XI, False)
            for h in HALVES:
                turn(dve, h, "D.addx")
                nc.vector.tensor_tensor(X[:, cols(h)], X[:, cols(h)], XN[:, cols(h)], ALU.add).then_inc(half[h], 1)
            for h in HALVES:
                turn(dve, h, "D.aff")
                nc.vector.tensor_scalar(XD4[:, :, 2 * h:2 * h + 2, :], XI[:, cols(h)].rearrange("p (i n b) -> p n i b", i=2, n=8),
                                        VEC[:, V_LW:V_LW + 1], VEC[:, V_LB:V_LB + 1], ALU.mult, ALU.add).then_inc(half[h], 1)
            nc.vector.memset(VD4[:, :, :, DH:DH + 1], 1.0).then_inc(d_one, 1)

            def d_evac(g):
                for w in range(1, 12, 2):
                    dve.wait_ge(d_p, 12 * g + w + 1)
                    if w < 8:
                        ins = nc.vector.tensor_copy(KD3[:, w - 1:w + 1, :].rearrange("p c t -> p (c t)"), PQ[:, 3, :])
                    else:
                        ins = nc.vector.tensor_copy(VD4[:, (2 * g + (w - 8) // 2) % 4, 8:16, 0:DH],
                                                    PQ[:, 3, :].rearrange("p (h k) -> p h k", k=DH))
                    ins.then_inc(d_vd, 1)

            X4 = X[:, :].rearrange("p (i b) -> p i b", i=4)
            for u in range(32 + 5):
                if u < 32:
                    if u % 8 == 0:
                        d_evac(u // 8)
                    mx = small[:, 64 + 4 * (u % 2):68 + 4 * (u % 2)]
                    s4 = PQ[:, u % 2, :].rearrange("p (i k) -> p i k", i=4)
                    dve.wait_ge(d_s, u + 1)
                    nc.vector.tensor_reduce(mx, s4, AXX, ALU.max).then_inc(d_mx, 1)
                    dve.wait_ge(d_mx, u + 1)
                    if u >= 2:
                        dve.wait_ge(d_t, d_job["p", u - 2] + 1)
                    nc.vector.tensor_tensor(PD4[:, u % 2, :, :], s4, mx.unsqueeze(2).to_broadcast([P, 4, P]),
                                            ALU.subtract).then_inc(d_sub, 1)
                if 0 <= u - 2 < 32:
                    v = u - 2
                    n = v // 4
                    rc = small[:, 72 + 4 * (v % 2):76 + 4 * (v % 2)]
                    o4 = PS[v % 2][:, 0:4 * (DH + 1)].rearrange("p (i k) -> p i k", i=4)
                    dve.wait_ge(d_o, v + 1)
                    nc.vector.reciprocal(rc.unsqueeze(2), o4[:, :, DH:DH + 1]).then_inc(d_rc, 1)
                    dve.wait_ge(d_rc, v + 1)
                    if n >= 2:
                        dve.wait_ge(d_t, d_job["o", n - 2, 1] + 1)
                    nc.vector.tensor_tensor(OD3[:, n % 2, :].rearrange("p (c r k) -> p r c k", r=2, k=DH)[:, v % 2, 4 * (v % 4 // 2):4 * (v % 4 // 2) + 4, :],
                                            o4[:, :, 0:DH], rc.unsqueeze(2).to_broadcast([P, 4, DH]), ALU.mult).then_inc(d_on, 1)
                if u >= 8 and u % 4 == 0:
                    n = u // 4 - 2
                    x4 = X4[:, :, 32 * n:32 * n + 32]
                    dve.wait_ge(d_wo, n + 1)
                    nc.vector.tensor_tensor(x4, x4, PQ[:, 2 + n % 2, 0:P].rearrange("p (i b) -> p i b", i=4), ALU.add).then_inc(d_res, 1)

            dve.wait_ge(d_res, 8)
            ln_dve(dve, "E", X, XN, False)
            nc.vector.memset(small[:, 40:48], 0.0).then_inc(cast, 1)
            dve.wait_ge(cast, 6)
            x_dve(dve, 1)
            for h in HALVES:
                turn(dve, h, "E.core")
                dve.wait_ge(x_at, 8 + 4 * (h + 1))
                nc.vector.memset(small[:, 48 + h:49 + h], 0.0).then_inc(half[h], 1)
            add_dve(dve, "E.oe", X, None, X)
            ln_dve(dve, "F", X, YF, False)
            nc.vector.memset(KPF, 0.0).then_inc(f_lv, 1)
            nc.vector.memset(VF4[:, :, :, DH:DH + 1], 1.0).then_inc(f_lv, 1)
            nc.vector.memset(PF3[:, :, SEGF:256], 0.0).then_inc(f_lv, 1)
            dve.wait_ge(f_lv, 3)
            dve.wait_ge(ld_lv, 16)
            dve.wait_ge(ld_fq, 32)

            def shift(p):
                y, xs = (z[:, cols(p)].rearrange("p (j t) -> p j t", j=2) for z in (YF, XSF))
                nc.vector.tensor_copy(xs[0:64], y[0:64])
                nc.vector.memset(xs[64:128, :, 0:1], 0.0)
                return nc.vector.tensor_copy(xs[64:128, :, 1:SEQ], y[64:128, :, 0:SEQ - 1])

            def f_project(p, layer, between):
                base = layer * 32 + 16 * p
                fturn(dve, p, layer, "shift")
                shift(p).then_inc(half[p], 1)
                if p == 0:
                    dve.wait_ge(f_add, base)
                    nc.vector.tensor_tensor(TABF, CST[:, C_ROT:C_ROT + 4 * P].rearrange("p (n q d) -> p n q d", n=4, q=2),
                                            LQ6[:, bass.ds(layer * (4 * DH), 4 * DH)].rearrange("p (n d) -> p n d", n=4)
                                            .unsqueeze(2).to_broadcast([P, 4, 2, DH]), ALU.mult).then_inc(f_tab, 1)
                    dve.wait_ge(f_tab, layer + 1)

                def inverse(j):
                    m = layer * 4 + (2 * p + j + 1)
                    nrm = NRM[:, :, 2 * j:2 * j + 2, :]
                    dve.wait_ge(f_nrm, m)
                    nc.vector.tensor_scalar(nrm, nrm, 1e-12, None, ALU.max).then_inc(f_gd, 1)
                    dve.wait_ge(f_gd, m)
                    nc.vector.reciprocal(NRC[:, :, 2 * j:2 * j + 2, :], nrm).then_inc(f_rc1, 1)

                for v in range(SLOTS):
                    n, w, c, i = slot_of(v)
                    if w < 2:
                        raw = PQ[:, v % 4, :]
                        t1 = (KN3, QN3)[w][:, n, c * 512:(c + 1) * 512].rearrange("p (h k) -> p h k", k=DH)
                        dve.wait_ge(f_sq, base + (i + 1))
                        nc.vector.tensor_reduce(NSQ[:, w, n, 8 * c:8 * c + 8], SQF3[:, i % 2, :].rearrange("p (h k) -> p h k", k=DH),
                                                AXX, ALU.add).then_inc(f_red, 1)
                        if v in ON_POOL:
                            dve.wait_ge(f_cp, copies(p, layer, v))
                        else:
                            if i >= 4:
                                dve.wait_ge(f_add, base + (i - 3))
                            nc.vector.tensor_tensor(T2F3[:, i % 4, :].rearrange("p (h s k) -> p h s k", s=2, k=DH // 2),
                                                    raw.rearrange("p (h s k) -> p h s k", s=2, k=DH // 2)[:, :, ::-1, :],
                                                    TABF[:, 2 * (1 - w) + 1, n % 2, :].rearrange("p (s k) -> p s k", s=2).unsqueeze(1)
                                                    .to_broadcast([P, 8, 2, DH // 2]), ALU.mult)
                        nc.vector.tensor_tensor(t1, raw.rearrange("p (h k) -> p h k", k=DH),
                                                TABF[:, 2 * (1 - w), n % 2, :].unsqueeze(1).to_broadcast([P, 8, DH]),
                                                ALU.mult).then_inc(f_t1, 1)
                    if v == 12:
                        inverse(0)
                    if v == 22:
                        inverse(1)
                    between(v)
            def f_core(p, layer):
                base = layer * 64 + 32 * p
                jbase = layer * 96 + 48 * p
                kbase = layer * 32 + 16 * p
                for u in range(32 + 4):
                    if u == 1:
                        fturn(dve, p, layer, "v")
                        dve.wait_ge(f_rc1, layer * 4 + (2 * p + 2))
                        dve.wait_ge(f_va, layer * 16 + (8 * p + 8))
                        nc.vector.memset(small[:, 48:49], 0.0).then_inc(half[p], 1)
                    if u < 32:
                        mx = small[:, 64 + 2 * (u % 2):66 + 2 * (u % 2)]
                        s2 = PQ[:, u % 2, 0:2 * SEGF].rearrange("p (q k) -> p q k", q=2)
                        dve.wait_ge(f_s, base + (u + 1))
                        nc.vector.tensor_reduce(mx, s2, AXX, ALU.max).then_inc(f_mx, 1)
                        dve.wait_ge(f_mx, base + (u + 1))
                        if u >= 3:
                            dve.wait_ge(f_t, jbase + (f_job["p", u - 3] + 1))
                        for q in range(2):
                            last = nc.vector.tensor_scalar(PFS(u % 3)[:, q, :], s2[:, q, :], mx[:, q:q + 1],
                                                           NRC[:, 1, 2 * (u // 16) + q, u % 16:u % 16 + 1], ALU.subtract, ALU.mult)
                        last.then_inc(f_sub, 1)
                    if u >= 4 and u % 2 == 0 and u - 3 < 32:
                        k = (u - 3) // 2
                        rc = small[:, 72 + 4 * (k % 2):76 + 4 * (k % 2)]
                        o4 = PQ[:, 2 + k % 2, 0:4 * (DH + 1)].rearrange("p (i k) -> p i k", i=4)
                        dve.wait_ge(f_o, base + (2 * k + 2))
                        nc.vector.reciprocal(rc.unsqueeze(2), o4[:, :, DH:DH + 1]).then_inc(f_rc, 1)
                        dve.wait_ge(f_rc, kbase + (k + 1))
                        if k >= 2:
                            dve.wait_ge(f_t, jbase + (f_job["o", k - 2] + 1))
                        nc.vector.tensor_tensor(ONF[:, k % 2, :, :].rearrange("p q (i k) -> p (q i) k", k=DH), o4[:, :, 0:DH],
                                                rc.unsqueeze(2).to_broadcast([P, 4, DH]), ALU.mult).then_inc(f_on, 1)
                fturn(dve, p, layer, "core")
                nc.vector.memset(small[:, 48:49], 0.0).then_inc(half[p], 1)

            def f_tail(name, p, layer):
                xs, y, xc = XSF[:, cols(p)], YF[:, cols(p)], XC[:, cols(p)]
                if name in ("woe", "shift2", "f.xc", "f.out", "aff", "w2e"):
                    fturn(dve, p, layer, name)
                if name == "woe":
                    nc.vector.tensor_tensor(y, y, PS[p][:, :], ALU.add).then_inc(half[p], 1)
                    if p == 0:
                        nc.vector.tensor_copy(LV[:, :], LV6[:, bass.ds(layer * NLV, NLV)]).then_inc(f_lv, 1)
                elif name == "shift2":
                    shift(p).then_inc(half[p], 1)
                elif name == "f.xc":
                    nc.vector.tensor_tensor(xc, xs, PS[p][:, :], ALU.subtract).then_inc(half[p], 1)
                elif name == "f.out":
                    nc.vector.tensor_tensor(xs, xc, RS[:, cols(p)], ALU.mult).then_inc(half[p], 1)
                elif name == "aff":
                    dve.wait_ge(f_lv, layer + 4)
                    nc.vector.tensor_scalar(xs, xs, LV[:, L_G:L_G + 1], LV[:, L_B:L_B + 1], ALU.mult, ALU.add).then_inc(half[p], 1)
                elif name.startswith("ffn"):
                    i = int(name[3])
                    m = min(P, GI - i * P)
                    dve.wait_ge(f_ge, layer * 6 + (3 * p + i + 1))
                    dve.wait_ge(f_a, layer * 6 + (3 * p + i + 1))
                    nc.vector.scalar_tensor_tensor(HF3[0:m, i, :], ffn_banks(p, i)[1][0:m, :], LV[0:m, L_B1A + i:L_B1A + i + 1], GF3[0:m, i, :],
                                                   ALU.add, ALU.mult).then_inc(f_hh, 1)
                    if i == GT - 1:
                        fturn(dve, p, layer, "ffn")
                        dve.wait_ge(f_hh, layer * 6 + (3 * p + 3))
                        nc.vector.memset(small[:, 48:49], 0.0).then_inc(half[p], 1)
                elif name == "w2e":
                    nc.vector.scalar_tensor_tensor(y, PS[p][:, :], LV[:, L_B2:L_B2 + 1], y, ALU.add, ALU.add).then_inc(half[p], 1)

            local_layers(dve, "dve", f_project, f_core, f_tail)
            for h in HALVES:
                dve.wait_ge(half[h], F_END)
                nc.vector.tensor_tensor(X[:, cols(h)], X[:, cols(h)], YF[:, cols(h)], ALU.add).then_inc(half[h], 1)


def kernel(**inputs):
    import numpy as np
    import concourse.bacc as _bacc
    from concourse import mybir as _mybir
    from concourse.bass_utils import run_bass_kernel_spmd as _run

    i = {k: np.asarray(v) for k, v in inputs.items()}
    f = np.float32

    def cols(*vs):
        return np.stack(vs, axis=1)

    cst = np.zeros((P, NCST), f)
    cst[:, C_ID:C_ID + P] = np.eye(P)
    cst[:, C_MEAN:C_MEAN + P] = 1.0 / P
    p = np.arange(P)
    cst[:, C_BLK:C_BLK + P] = (p[:, None] // DH == p[None, :] // DH)
    cst[:, C_HM:C_HM + AH] = (p[:, None] // ADK == np.arange(AH)[None, :])
    cst[:, C_PR:C_PR + 4 * NE] = np.tile(NE - np.arange(NE), 4)[None, :]
    cst[:, C_MD:C_MD + P] = np.where(p[:, None] % 32 == p[None, :] % 32, 0.0, -1e30)
    for q in range(2):
        it = q * P + p[:, None]
        jt = q * P - WIN + np.arange(SEGF)[None, :]
        ok = (jt >= 0) & (it >= jt) & (it <= jt + WIN)
        cst[:, C_MF + q * SEGF:C_MF + (q + 1) * SEGF] = np.where(ok, 0.0, -1e30)
    hd = np.arange(0, DH, 2, dtype=f)
    inv = (1.0 / f(10000.0) ** (hd / f(DH))).astype(f)
    t = np.arange(SEQ, dtype=f)
    fr = (t[:, None] * inv[None, :]).astype(f)
    base = ((hd + f(0.4 * DH)) / f(1.4 * DH)).astype(f)
    sc = (base[None, :] ** ((t - SEQ // 2) / f(WIN // 2))[:, None]).astype(f)
    fr, sc = (np.concatenate([z, z], 1) for z in (fr, sc))
    sign = np.where(np.arange(DH) < DH // 2, -1.0, 1.0).astype(f)
    rot = [np.cos(fr) * sc, np.sin(fr) * sc * sign, np.cos(fr) / sc, np.sin(fr) / sc * sign]
    for n, r in enumerate(rot):
        cst[:, C_ROT + n * P:C_ROT + (n + 1) * P] = r.reshape(2, P, DH).transpose(1, 0, 2).reshape(P, P)

    vec = np.zeros((P, NVEC), f)
    for c, n in ((V_BQ, 'L0_attn_bq'), (V_BK, 'L0_attn_bk'), (V_BV, 'L0_attn_bv'), (V_HB, 'L0_xattn_hb'), (V_QB, 'L0_xattn_qb'),
                 (V_KB, 'L0_xattn_kb'), (V_CB, 'L0_xattn_cb'), (V_VB, 'L0_xattn_vb'), (V_OB, 'L0_xattn_ob'),
                 (V_LW, 'L1_attn_ln_w'), (V_LB, 'L1_attn_ln_b')):
        vec[:, c] = i[n]
    vec[:, V_EG:V_EG + NE] = i['L0_ffn_ln_g'].T
    vec[:, V_EB:V_EB + NE] = i['L0_ffn_ln_b'].T
    vec[:, V_EB2:V_EB2 + NE] = i['L0_ffn_b2'].T
    vec[:, V_EB1:] = i['L0_ffn_b1'].reshape(NE * FT, P).T
    rel = i['L0_attn_rel_emb'][:, ::-1]
    band = P - 1 - p[:, None] + np.arange(3 * P)[None, :]
    band = np.minimum(band, 2 * SEQ - 2)
    x = i['L0_xattn_hW'], i['L0_xattn_qW'], i['L0_xattn_kW'], i['L0_xattn_cW'], i['L0_xattn_vW'], i['L0_xattn_oW']
    wd = i['L1_attn_w_qkv'].reshape(NH, 3, DH, P).transpose(3, 1, 0, 2).reshape(P, 3 * NH * DH)
    wdo = i['L1_attn_w_out'].T.reshape(CH, P, P).transpose(1, 0, 2).reshape(P, CH * P)
    wq = i['L1_ffn_Wqkv']
    lvec = np.zeros((DEPTH, P, NLV), f)
    lvec[:, :, L_G], lvec[:, :, L_B], lvec[:, :, L_B2] = i['L1_ffn_ln_g'], i['L1_ffn_ln_b'], i['L1_ffn_b2']
    b1 = np.zeros((DEPTH, 2, GT * P), f)
    b1[:, :, :GI] = i['L1_ffn_b1'].reshape(DEPTH, 2, GI)
    lvec[:, :, L_B1A:L_B1A + 2 * GT] = b1.reshape(DEPTH, 2 * GT, P).transpose(0, 2, 1)
    qs, ks = i['L1_ffn_q_scale'], i['L1_ffn_k_scale']
    half_swap = (np.arange(DH) + DH // 2) % DH
    scales = np.stack([qs, qs[:, half_swap], ks, ks[:, half_swap]], 1)
    w2 = np.zeros((DEPTH, GT * P, P), f)
    w2[:, :GI] = i['L1_ffn_W2']
    arrays = {
        "xT": i['x'].reshape(T, P).T, "cst": cst, "vec": vec,
        "wa": np.concatenate([i['L0_attn_Wq'], i['L0_attn_Wk'], i['L0_attn_Wv']], 1),
        "rel": rel[:, band].transpose(1, 0, 2).reshape(P, -1),
        "ctxT": i['ctx_1024'].transpose(2, 0, 1).reshape(P, -1), "ctxN": i['ctx_1024'],
        "wb": np.concatenate([x[0].T, x[1].T, x[2], x[3], x[3].T, x[4].T, x[5].T], 1),
        "cen": i['L0_ffn_centroids'].T,
        "we1": i['L0_ffn_W1'].transpose(1, 0, 2).reshape(P, -1),
        "we2": i['L0_ffn_W2'].reshape(NE, FT, P, P).transpose(2, 0, 1, 3).reshape(P, -1),
        "wd": np.concatenate([wd, wdo], 1),
        "we": np.concatenate([i['L1_xattn_Wq'].T, i['L1_xattn_Wk'], i['L1_xattn_Wv'].T, i['L1_xattn_Wo'].T], 1),
        "lvec": lvec,
        "wfq": wq,
        "scl": np.broadcast_to(scales.reshape(1, -1), (P, DEPTH * 4 * DH)),
        "wfo": i['L1_ffn_Wo'].reshape(DEPTH, CH, P, P).transpose(0, 2, 1, 3).reshape(DEPTH, P, CH * P),
        "wf1": i['L1_ffn_W1'],
        "wf2": w2.reshape(DEPTH, GT, P, P).transpose(0, 2, 1, 3).reshape(DEPTH, P, GT * P),
    }
    nc = _bacc.Bacc("TRN2", target_bir_lowering=False, num_devices=1)
    given, args = {}, []
    for name, arr in arrays.items():
        arr = np.ascontiguousarray(arr)
        given[f"in_{name}"] = arr
        args.append(nc.dram_tensor(f"in_{name}", arr.shape, _mybir.dt.from_np(arr.dtype), kind="ExternalInput").ap())
    outT = nc.dram_tensor("out_T", (P, T), F32, kind="ExternalOutput").ap()
    decoder(nc, *args, outT)
    r = _run(nc, [given], core_ids=[0])
    return np.ascontiguousarray(r.results[0]["out_T"].T).reshape(NB, SEQ, P)
```
